# Optimizing a Trainium2 kernel written in Bass

```python
import numpy as np
import jax
import jax.numpy as jnp

def _softmax(x, axis=-1):
    return jax.nn.softmax(x, axis=axis)

def _gelu(x):
    return jax.nn.gelu(x, approximate=True)

def _silu(x):
    return jax.nn.silu(x)

def _sigmoid(x):
    return jax.nn.sigmoid(x)

def _layernorm(x, axis=-1, eps=1e-05):
    m = jnp.mean(x, axis=axis, keepdims=True)
    v = jnp.var(x, axis=axis, keepdims=True)
    return (x - m) / jnp.sqrt(v + eps)

def _scatter_add(tgt, idx, src, axis=0):
    return tgt.at[idx].add(src)

def _segment_sum(src, seg, n):
    return jax.ops.segment_sum(src, seg, n)
kernel_name = 'mk_seq_preln_d1_jaxref_r8_41d28f'

def setup_inputs(seed: int=0):
    np.random.seed(seed)
    _w = jnp.asarray

    def _L0_attn_setup():
        import jax, jax.numpy as jnp
        import numpy as np
        EMBED_DIM = 128
        NUM_HEADS = 8
        NUM_POINTS = 4
        B, N = (4, 1024)
        key = jax.random.key(seed)
        ks = jax.random.split(key, 8)
        C, H, P = (EMBED_DIM, NUM_HEADS, NUM_POINTS)
        sc = 1.0 / np.sqrt(C)
        x = jax.random.normal(ks[0], (B, N, C), dtype=jnp.float32)
        W_off = jax.random.normal(ks[1], (C, H * P * 2), dtype=jnp.float32) * sc
        b_off = jax.random.normal(ks[2], (H * P * 2,), dtype=jnp.float32) * 0.1
        W_attn = jax.random.normal(ks[3], (C, H * P), dtype=jnp.float32) * sc
        b_attn = jax.random.normal(ks[4], (H * P,), dtype=jnp.float32) * 0.1
        W_out = jax.random.normal(ks[5], (C, C), dtype=jnp.float32) * sc
        b_out = jax.random.normal(ks[6], (C,), dtype=jnp.float32) * 0.1
        return {'x': x, 'W_off': W_off, 'b_off': b_off, 'W_attn': W_attn, 'b_attn': b_attn, 'W_out': W_out, 'b_out': b_out}
    _L0_attn_in = _L0_attn_setup()

    def _L0_ffn_setup():
        import jax, jax.numpy as jnp
        import numpy as np
        B, S, D, M, E, K = (2, 256, 128, 176, 8, 2)
        key = jax.random.key(seed)
        k0, k1, k2, k3, k4 = jax.random.split(key, 5)
        scale = 0.02
        return {'x': jax.random.normal(k0, (B, S, D), dtype=jnp.float32), 'w_gate': jax.random.normal(k1, (D, E), dtype=jnp.float32) * scale, 'w_g': jax.random.normal(k2, (E, D, M), dtype=jnp.float32) * scale, 'w_u': jax.random.normal(k3, (E, D, M), dtype=jnp.float32) * scale, 'w_d': jax.random.normal(k4, (E, M, D), dtype=jnp.float32) * scale}
    _L0_ffn_in = _L0_ffn_setup()
    _d = {'L0_attn_x': _L0_attn_in['x'], 'L0_attn_W_off': _L0_attn_in['W_off'], 'L0_attn_b_off': _L0_attn_in['b_off'], 'L0_attn_W_attn': _L0_attn_in['W_attn'], 'L0_attn_b_attn': _L0_attn_in['b_attn'], 'L0_attn_W_out': _L0_attn_in['W_out'], 'L0_attn_b_out': _L0_attn_in['b_out'], 'L0_ffn_w_gate': _L0_ffn_in['w_gate'], 'L0_ffn_w_g': _L0_ffn_in['w_g'], 'L0_ffn_w_u': _L0_ffn_in['w_u'], 'L0_ffn_w_d': _L0_ffn_in['w_d']}
    _x0 = _d['L0_attn_x']
    _d['L0_attn_x'] = jax.random.normal(jax.random.fold_in(jax.random.key(seed), 1), (4, 512, 128), dtype=_x0.dtype)
    del _x0
    return _d

def reference(L0_attn_x, L0_attn_W_off, L0_attn_b_off, L0_attn_W_attn, L0_attn_b_attn, L0_attn_W_out, L0_attn_b_out, L0_ffn_w_gate, L0_ffn_w_g, L0_ffn_w_u, L0_ffn_w_d):

    def _L0_attn_ref(x, W_off, b_off, W_attn, b_attn, W_out, b_out):
        import jax, jax.numpy as jnp
        import numpy as np
        EMBED_DIM = 128
        NUM_HEADS = 8
        NUM_POINTS = 4
        B, N = (4, 1024)
        Bx, Nx, C = x.shape
        H, P = (NUM_HEADS, NUM_POINTS)
        off = (x @ W_off + b_off).reshape(Bx, Nx, H, P, 2)
        w = jax.nn.softmax((x @ W_attn + b_attn).reshape(Bx, Nx, H, P), axis=-1)
        idx = off[..., 0].astype(jnp.int32)
        idx = jnp.where(idx < 0, idx + C, idx)
        idx = jnp.clip(idx, 0, C - 1)
        x0 = x[:, 0, :]
        g = jnp.take_along_axis(x0, idx.reshape(Bx, -1), axis=1).reshape(Bx, Nx, H, P)
        s = jnp.sum(g * w, axis=(2, 3))
        out = jnp.broadcast_to(s[..., None], (Bx, Nx, C))
        return out @ W_out + b_out

    def _L0_ffn_ref(x, w_gate, w_g, w_u, w_d):
        import jax, jax.numpy as jnp
        import numpy as np
        B, S, D, M, E, K = (2, 256, 128, 176, 8, 2)
        scores = x @ w_gate
        topk_scores, topk_idx = jax.lax.top_k(scores, K)
        topk_probs = jax.nn.softmax(topk_scores, axis=-1)
        gating = jnp.sum(jax.nn.one_hot(topk_idx, E, dtype=topk_probs.dtype) * topk_probs[..., None], axis=-2)
        hidden = jax.nn.silu(jnp.einsum('bsd,edm->ebsm', x, w_g)) * jnp.einsum('bsd,edm->ebsm', x, w_u)
        expert_out = jnp.einsum('ebsm,emd->ebsd', hidden, w_d)
        y = jnp.einsum('bse,ebsd->bsd', gating, expert_out)
        return y
    x = L0_attn_x
    x = x + _L0_attn_ref(_layernorm(x, axis=-1), L0_attn_W_off, L0_attn_b_off, L0_attn_W_attn, L0_attn_b_attn, L0_attn_W_out, L0_attn_b_out)
    x = x + _L0_ffn_ref(_layernorm(x, axis=-1), L0_ffn_w_gate, L0_ffn_w_g, L0_ffn_w_u, L0_ffn_w_d)
    return x

_drawn_inputs = setup_inputs


def setup_inputs(seed=0):
    import zlib

    import numpy as np

    out = dict(_drawn_inputs(seed))
    spreads = {}
    factors = {'L0_attn_b_attn': 4.986,
     'L0_attn_b_out': 5.002,
     'L0_ffn_w_gate': 8.0,
     'L0_ffn_w_g': 8.0,
     'L0_ffn_w_u': 8.0,
     'L0_ffn_w_d': 8.0}
    for name, (base, spread) in spreads.items():
        noise = np.random.default_rng([zlib.crc32(name.encode()), seed]).standard_normal(out[name].shape)
        drawn = base * np.exp(spread * noise) if base else spread * noise
        out[name] = jnp.asarray(drawn.astype(out[name].dtype))
    for name, factor in factors.items():
        out[name] = (out[name] * factor).astype(out[name].dtype)
    return out
```

```python
import concourse.bass as bass
from concourse import mybir
from contextlib import ExitStack


def deform_attn_then_moe(nc, x, w_off, b_off, w_attn, b_attn, w_out, b_out, w_gate, w_g, w_u, w_d, out):
    fp32, fp32r, bf16, i32 = (mybir.dt.float32, mybir.dt.float32r, mybir.dt.bfloat16, mybir.dt.int32)
    ALU = mybir.AluOpType
    ACT = mybir.ActivationFunctionType
    AX = mybir.AxisListType

    B, N, C = x.shape
    P = 128
    T = N // P
    NE, _, FM = w_g.shape
    HALL = NE * FM
    M = HALL // P
    HP = w_attn.shape[1]
    NP = 4
    NHD = HP // NP
    LO, HI = 16, C // 16
    QL = HP // (P // LO)
    QH = HP // (P // HI)
    JL, JH = P // LO, P // HI
    PIECES = 3
    GK = PIECES * NE
    EPS = 1e-5
    LOWEST = -3.0e38
    LAG = 2
    NH = 3

    w_g_v = w_g.rearrange("e d m -> d e m")
    w_u_v = w_u.rearrange("e d m -> d e m")
    w_d_v = w_d.rearrange("e m d -> (e m) d").rearrange("(c p) d -> p c d", p=P)

    ctx = ExitStack()
    with ctx:
        def sb(name, shape, dt=fp32):
            return ctx.enter_context(nc.sbuf_tensor(name, shape, dt))

        def sem(name):
            return ctx.enter_context(nc.semaphore(name))

        xs = sb("xs", [P, B * T, C])
        xb = sb("xb", [P, B * T, C])
        x2 = sb("x2", [P, B * T, C])
        wp = sb("wp", [P, 3 * HP])
        bp = sb("bp", [P, 3 * HP])
        wcat = sb("wcat", [P, 2 * HP])
        bcat = sb("bcat", [P, 2 * HP])
        wo = sb("wo", [P, C])
        bo = sb("bo", [P, C])
        cw = sb("cw", [P, C])
        wgt = sb("wgt", [P, NE])
        wgt_hi = sb("wgt_hi", [P, NE], fp32r)
        wgt_lo = sb("wgt_lo", [P, NE], fp32r)
        raw = sb("raw", [P, 3, HALL])
        whi = sb("whi", [P, 3, HALL], fp32r)
        wlo = sb("wlo", [P, 3, HALL], fp32r)
        ones = sb("ones", [P, P])
        ident = sb("ident", [P, P])
        identb = sb("identb", [P, P], bf16)
        part = sb("part", [P, 1], i32)
        bits = sb("bits", [P, 4], i32)
        col = sb("col", [P, 4])
        row_i = sb("row_i", [P, 16], i32)
        row_lo = sb("row_lo", [P, JL, LO], i32)
        row_e = sb("row_e", [GK, HALL], i32)
        rank = sb("rank", [P, NE])
        rank_i = sb("rank_i", [P, NE], i32)
        sel_lo = sb("sel_lo", [P, P])
        own_hi = sb("own_hi", [P, HI])
        sum_hi = sb("sum_hi", [P, JH])
        spread = sb("spread", [GK, HALL], bf16)
        mhalf = sb("mhalf", [P, T])
        st6 = sb("st6", [P, B * T, 6])
        mv = sb("mv", [P, B * T, 2])
        ve = sb("ve", [P, B * T])
        rs = sb("rs", [P, B * T])
        xn = sb("xn", [P, B * T, C])
        xnT = sb("xnT", [P, B, N])
        pr = sb("pr", [P, B * T, 2 * HP])
        mx = sb("mx", [P, B, T * NHD])
        ex = sb("ex", [P, B, T * HP])
        sm = sb("sm", [P, B, T * NHD])
        wt = sb("wt", [P, B, T * HP])
        ia = sb("ia", [P, T, HP])
        ii = sb("ii", [P, T, HP], i32)
        ig = sb("ig", [P, T, HP])
        fl = sb("fl", [P, T, HP])
        ng = sb("ng", [P, T, HP])
        cc = sb("cc", [P, T, HP])
        ix = sb("ix", [P, T, HP], i32)
        ih = sb("ih", [P, T, HP], i32)
        lh = sb("lh", [P, B * T, 2 * HP], bf16)
        lhT = sb("lhT", [2 * HP, B, N], bf16)
        rep_lo = sb("rep_lo", [P, B, QL, N], bf16)
        rep_hi = sb("rep_hi", [P, B, QH, N], bf16)
        tv = sb("tv", [P, B, HI])
        t3 = sb("t3", [P, PIECES, HI], bf16)
        tr = sb("tr", [P, 3, HI])
        tbd = sb("tbd", [P, B, PIECES, JL, HI], bf16)
        oh = sb("oh", [P, QL, N], bf16)
        ar = sb("ar", [P, QH, N])
        gw = sb("gw", [P, T, HP])
        ss = sb("ss", [P, B * T])
        st6b = sb("st6b", [P, B * T, 6])
        mvb = sb("mvb", [P, B * T, 2])
        veb = sb("veb", [P, B * T])
        rsb = sb("rsb", [P, B * T])
        xn2 = sb("xn2", [P, T, C])
        xhi = sb("xhi", [P, 2, N], fp32r)
        xlo = sb("xlo", [P, 2, N], fp32r)
        sc = sb("sc", [P, T, NE])
        tk = sb("tk", [P, 8, T, NE])
        tm = sb("tm", [P, 8, T])
        g3 = sb("g3", [P, T, PIECES, NE], bf16)
        gT = sb("gT", [GK, 2, N], bf16)
        sg = sb("sg", [P, 2, N])
        su = sb("su", [P, 2, N])
        hh = sb("hh", [P, NH, N])
        hhi = sb("hhi", [P, NH, N], fp32r)
        hlo = sb("hlo", [P, NH, N], fp32r)
        ys = sb("ys", [P, N])
        yo = sb("yo", [P, B * T, C])

        def bank(name):
            return ctx.enter_context(nc.psum_tensor(name, [P, 512], fp32))

        ps_g = [bank("ps_g0"), bank("ps_g1")]
        ps_u = [bank("ps_u0"), bank("ps_u1")]
        ps_w, ps_y, ps_a, ps_b = bank("ps_w"), bank("ps_y"), bank("ps_a"), bank("ps_b")

        ld_x = [sem(f"ld_x{b}") for b in range(B)]
        ld_p, ld_o, ld_g, ld_w = sem("ld_p"), sem("ld_o"), sem("ld_g"), [sem(f"ld_w{i}") for i in range(3)]
        st_out = sem("st_out")
        pool_c, dve_c, wcat_ok, whi_ok, wlo_ok, cwp_ok, cw_ok, xb_ok, wgt_ok = map(
            sem, ["pool_c", "dve_c", "wcat_ok", "whi_ok", "wlo_ok", "cwp_ok", "cw_ok", "xb_ok", "wgt_ok"])
        dve = sem("dve")
        pool = sem("pool")
        (var_ok, rs_ok, xn_ok, xnp_ok, xnT_ok, prp_ok, pr_ok, sub_ok, exp_ok, tv_ok, tp_ok, tbd_ok, lh_ok,
         lhp_ok, lhT_ok, oh_ok, look_ok, pick_ok, got_ok, gw_ok) = map(sem, [
             "var_ok", "rs_ok", "xn_ok", "xnp_ok", "xnT_ok", "prp_ok", "pr_ok", "sub_ok", "exp_ok", "tv_ok",
             "tp_ok", "tbd_ok", "lh_ok", "lhp_ok", "lhT_ok", "oh_ok", "look_ok", "pick_ok", "got_ok", "gw_ok"])
        ld_rep = [sem(f"ld_rep{b}") for b in range(B)]
        (varb_ok, rsb_ok, xn2_ok, xn2p_ok, xhi_ok, xlo_ok, scp_ok, sc_ok, gap_ok, th_ok, g3_ok, gTp_ok, gT_ok,
         y_ok, yp_ok, out_ok) = map(sem, [
             "varb_ok", "rsb_ok", "xn2_ok", "xn2p_ok", "xhi_ok", "xlo_ok", "scp_ok", "sc_ok", "gap_ok", "th_ok",
             "g3_ok", "gTp_ok", "gT_ok", "y_ok", "yp_ok", "out_ok"])
        (pg_ok, pu_ok, pw_ok, sg_ok, su_ok, hh_ok, hhi_ok, hlo_ok, dn_ok) = map(sem, [
            "pg_ok", "pu_ok", "pw_ok", "sg_ok", "su_ok", "hh_ok", "hhi_ok", "hlo_ok", "dn_ok"])

        block = ctx.enter_context(nc.Block())

        @block.sync
        def _(sp):
            xv = x.rearrange("b (t p) c -> b p t c", p=P)
            sp.dma_start(xs[:, 0:T, :], xv[0]).then_inc(ld_x[0], 16)
            sp.dma_start(wp[:, 0:2 * HP], w_off).then_inc(ld_p, 16)
            sp.dma_start(wp[:, 2 * HP:3 * HP], w_attn).then_inc(ld_p, 16)
            for b in range(1, B):
                sp.dma_start(xs[:, b * T:(b + 1) * T, :], xv[b]).then_inc(ld_x[b], 16)
            sp.dma_start(raw[:, 0, :].rearrange("p (e m) -> p e m", e=NE), w_g_v).then_inc(ld_w[0], 16)
            sp.dma_start(raw[:, 1, :].rearrange("p (e m) -> p e m", e=NE), w_u_v).then_inc(ld_w[1], 16)
            sp.dma_start(raw[:, 2, :].rearrange("p (c d) -> p c d", c=M), w_d_v).then_inc(ld_w[2], 16)
            for b in range(B):
                sp.wait_ge(lhT_ok, b + 1)
                for q in range(QL):
                    sp.dma_start(rep_lo[:, b, q, :],
                                 lhT[q * JL:(q + 1) * JL, b, :].unsqueeze(1).to_broadcast([JL, LO, N])
                                 ).then_inc(ld_rep[b], 16)
                for q in range(QH):
                    sp.dma_start(rep_hi[:, b, q, :],
                                 lhT[HP + q * JH:HP + (q + 1) * JH, b, :].unsqueeze(1).to_broadcast([JH, HI, N])
                                 ).then_inc(ld_rep[b], 16)
            ov = out.rearrange("b (t p) c -> b p t c", p=P)
            for b in range(B):
                sp.wait_ge(out_ok, b + 1)
                sp.dma_start(ov[b], yo[:, b * T:(b + 1) * T, :]).then_inc(st_out, 16)
            sp.wait_ge(st_out, 16 * B)

        @block.gpsimd
        def _(eng):
            n = [0]

            def link(ins):
                n[0] += 1
                ins.then_inc(pool, 1)
                eng.wait_ge(pool, n[0])

            eng.memset(mhalf[:, :], -0.5).then_inc(pool_c, 1)
            eng.iota(part[:, :], pattern=[[0, 1]], base=0, channel_multiplier=1).then_inc(pool_c, 1)
            eng.iota(row_i[:, :], pattern=[[1, 16]], base=0, channel_multiplier=0).then_inc(pool_c, 1)
            eng.memset(ident[:, :], 0.0).then_inc(pool_c, 1)
            eng.wait_ge(pool_c, 4)
            eng.affine_select(out=ident[:, :], in_=ident[:, :], compare_op=ALU.not_equal, fill=1.0, base=0,
                              pattern=[[-1, P]], channel_multiplier=1).then_inc(pool_c, 1)
            eng.iota(row_lo[:, :, :], pattern=[[0, JL], [1, LO]], base=0, channel_multiplier=0).then_inc(pool_c, 1)
            eng.memset(ones[:, :], 1.0).then_inc(pool_c, 1)
            eng.iota(rank_i[:, :], pattern=[[-1, NE]], base=NE, channel_multiplier=0).then_inc(pool_c, 1)
            eng.iota(row_e[:, :], pattern=[[1, NE], [0, FM]], base=0, channel_multiplier=0).then_inc(pool_c, 1)

            def rstd(v, m, r, b, ready, done):
                t = slice(b * T, (b + 1) * T)
                eng.wait_ge(ready, b + 1)
                link(eng.tensor_scalar(v[:, t], m[:, t, 1], EPS, None, ALU.add))
                eng.tensor_tensor(r[:, t], v[:, t], mhalf[:, :], ALU.pow).then_inc(done, 1)

            for b in range(B):
                rstd(ve, mv, rs, b, var_ok, rs_ok)
                if b == 0:
                    eng.wait_ge(ld_o, 48)
                t = slice(b * T, (b + 1) * T)
                eng.wait_ge(ld_x[b], 16)
                eng.tensor_tensor(xb[:, t, :], xs[:, t, :], bo[:, :].unsqueeze(1).to_broadcast([P, T, C]),
                                  ALU.add).then_inc(xb_ok, 1)
                if b < 3:
                    eng.wait_ge(whi_ok, b + 1)
                    eng.tensor_tensor(wlo[:, b, :], raw[:, b, :], whi[:, b, :].bitcast(fp32), ALU.subtract
                                      ).then_inc(wlo_ok, 1)
                if b == 0:
                    rstd(veb, mvb, rsb, 0, varb_ok, rsb_ok)
            for b in range(B):
                for m in range(M):
                    k = b * M + m
                    eng.wait_ge(hhi_ok, k + 1)
                    if k >= NH:
                        eng.wait_ge(dn_ok, k - NH + 1)
                    eng.tensor_tensor(hlo[:, k % NH, :], hh[:, k % NH, :], hhi[:, k % NH, :].bitcast(fp32),
                                      ALU.subtract).then_inc(hlo_ok, 1)
                    if m == 5 and b + 1 < B:
                        rstd(veb, mvb, rsb, b + 1, varb_ok, rsb_ok)

        @block.scalar
        def _(act):
            act.dma_start(bp[:, 0:2 * HP], b_off.partition_broadcast(P)).then_inc(ld_p, 16)
            act.dma_start(bp[:, 2 * HP:3 * HP], b_attn.partition_broadcast(P)).then_inc(ld_p, 16)
            act.dma_start(wo[:, :], w_out).then_inc(ld_o, 16)
            act.dma_start(bo[:, :], b_out.partition_broadcast(P)).then_inc(ld_o, 16)
            act.dma_start(wgt[:, :], w_gate).then_inc(ld_o, 16)

            def att_exp(b):
                act.wait_ge(sub_ok, b + 1)
                nc.scalar.activation(ex[:, b, :], ex[:, b, :], ACT.Exp).then_inc(exp_ok, 1)

            def x_hi(b):
                act.wait_ge(xn2p_ok, b + 1)
                if b >= 2:
                    act.wait_ge(pu_ok, M * (b - 1))
                nc.scalar.activation(xhi[:, b % 2, :], ps_a[:, :], ACT.Copy).then_inc(xhi_ok, 1)

            def split(b):
                act.wait_ge(gap_ok, b + 1)
                nc.scalar.activation(tm[:, 6, :], tm[:, 5, :], ACT.Tanh, scale=0.5).then_inc(th_ok, 1)

            def gates_T(b):
                act.wait_ge(gTp_ok, b + 1)
                if b >= 2:
                    act.wait_ge(pw_ok, M * (b - 1))
                nc.scalar.activation(gT[:, b % 2, :], ps_b[0:GK, 0:256].bitcast(bf16), ACT.Copy).then_inc(gT_ok, 1)

            def front(b):
                act.wait_ge(xnp_ok, b + 1)
                nc.scalar.activation(xnT[:, b, :], ps_g[b % 2][:, :], ACT.Copy).then_inc(xnT_ok, 1)
                act.wait_ge(lhp_ok, b + 1)
                nc.scalar.activation(lhT[:, b, :], ps_u[b % 2][0:2 * HP, 256:512].bitcast(bf16), ACT.Copy
                                     ).then_inc(lhT_ok, 1)
                att_exp(b)
                if b < 3:
                    act.wait_ge(ld_w[b], 16)
                    nc.scalar.activation(whi[:, b, :], raw[:, b, :], ACT.Copy).then_inc(whi_ok, 1)

            front(0)
            front(1)
            x_hi(0)
            front(2)
            split(0)
            gates_T(0)
            front(3)
            for b in range(B):
                for m in range(M):
                    k = b * M + m
                    act.wait_ge(pg_ok, k + 1)
                    if k >= 2:
                        act.wait_ge(su_ok, k - 1)
                    nc.scalar.activation(sg[:, k % 2, :], ps_g[k % 2][:, :], ACT.Silu).then_inc(sg_ok, 1)
                    if m == 1 and b >= 1:
                        act.wait_ge(dn_ok, M * b)
                        if b >= 2:
                            act.wait_ge(yp_ok, b - 1)
                        nc.scalar.activation(ys[:, :], ps_y[:, :], ACT.Copy).then_inc(y_ok, 1)
                    if k >= 1:
                        j = k - 1
                        act.wait_ge(hh_ok, j + 1)
                        if j >= NH:
                            act.wait_ge(dn_ok, j - NH + 1)
                        nc.scalar.activation(hhi[:, j % NH, :], hh[:, j % NH, :], ACT.Copy).then_inc(hhi_ok, 1)
                    if b + 1 < B:
                        if m == 7:
                            x_hi(b + 1)
                        if m == 9:
                            split(b + 1)
                        if m == 10:
                            gates_T(b + 1)
            j = B * M - 1
            act.wait_ge(hh_ok, j + 1)
            act.wait_ge(dn_ok, j - NH + 1)
            nc.scalar.activation(hhi[:, j % NH, :], hh[:, j % NH, :], ACT.Copy).then_inc(hhi_ok, 1)
            act.wait_ge(dn_ok, M * B)
            act.wait_ge(yp_ok, B - 1)
            nc.scalar.activation(ys[:, :], ps_y[:, :], ACT.Copy).then_inc(y_ok, 1)

        @block.vector
        def _(eng):
            n = [0]
            V = nc.vector

            def link(ins):
                n[0] += 1
                ins.then_inc(dve, 1)
                eng.wait_ge(dve, n[0])

            eng.wait_ge(ld_p, 64)
            V.tensor_copy(wcat[:, 0:HP], wp[:, 0:2 * HP:2]).then_inc(wcat_ok, 1)
            V.tensor_copy(wcat[:, HP:2 * HP], wp[:, 2 * HP:3 * HP]).then_inc(wcat_ok, 1)
            V.tensor_copy(bcat[:, 0:HP], bp[:, 0:2 * HP:2])
            link(V.tensor_copy(bcat[:, HP:2 * HP], bp[:, 2 * HP:3 * HP]))
            eng.wait_ge(pool_c, 9)
            V.tensor_copy(identb[:, :], ident[:, :])
            V.tensor_copy(rank[:, :], rank_i[:, :])
            for i, (op, v) in enumerate([(ALU.bitwise_and, LO - 1), (ALU.bitwise_and, HI - 1),
                                         (ALU.arith_shift_right, 4), (ALU.arith_shift_right, 3)]):
                ins = V.tensor_scalar(bits[:, i:i + 1], part[:, :], v, None, op)
            link(ins)
            link(V.tensor_copy(col[:, :], bits[:, :]))
            V.tensor_scalar(sel_lo[:, :].rearrange("p (j b) -> p j b", b=LO), row_lo[:, :, :], col[:, 0:1], None,
                            ALU.is_equal)
            V.tensor_scalar(own_hi[:, :], row_i[:, 0:HI], col[:, 2:3], None, ALU.is_equal)
            V.tensor_scalar(sum_hi[:, :], row_i[:, 0:JH], col[:, 3:4], None, ALU.is_equal)
            V.tensor_scalar(spread[:, :], row_e[:, :], col[0:GK, 1:2], None, ALU.is_equal).then_inc(dve_c, 1)

            def split_gate():
                eng.wait_ge(ld_o, 48)
                V.tensor_copy(wgt_hi[:, :], wgt[:, :]).then_inc(wgt_ok, 1)
                eng.wait_ge(wgt_ok, 1)
                V.tensor_tensor(wgt_lo[:, :], wgt[:, :], wgt_hi[:, :].bitcast(fp32), ALU.subtract).then_inc(wgt_ok, 1)

            def stats(src, s6, m2, b, done):
                for t in range(b * T, (b + 1) * T):
                    ins = V.bn_stats(s6[:, t, :], src[:, t, :])
                link(ins)
                for t in range(b * T, (b + 1) * T):
                    ins = V.bn_aggr(m2[:, t, :], s6[:, t, :])
                ins.then_inc(done, 1)

            def normalise(dst, src, m2, r, b, ready, done):
                eng.wait_ge(ready, b + 1)
                for t in range(b * T, (b + 1) * T):
                    ins = V.tensor_scalar(dst[:, t % dst.shape[1], :], src[:, t, :], m2[:, t, 0:1], r[:, t:t + 1],
                                          ALU.subtract, ALU.mult)
                ins.then_inc(done, 1)

            def project(b):
                t = slice(b * T, (b + 1) * T)
                eng.wait_ge(prp_ok, b + 1)
                V.tensor_tensor(pr[:, t, :], ps_u[b % 2][:, 0:T * 2 * HP].rearrange("p (t n) -> p t n", t=T),
                                bcat[:, :].unsqueeze(1).to_broadcast([P, T, 2 * HP]), ALU.add).then_inc(pr_ok, 1)
                eng.wait_ge(pr_ok, b + 1)

            def weights_in(b):
                t = slice(b * T, (b + 1) * T)
                logits = pr[:, t, HP:2 * HP].rearrange("p t (h q) -> p t h q", q=NP)
                m4 = mx[:, b, :].rearrange("p (t h) -> p t h", t=T)
                link(V.tensor_reduce(m4, logits, AX.X, ALU.max))
                V.tensor_tensor(ex[:, b, :].rearrange("p (t h q) -> p t h q", t=T, q=NP), logits,
                                m4.unsqueeze(3).to_broadcast([P, T, NHD, NP]), ALU.subtract).then_inc(sub_ok, 1)

            def weights_out(b):
                eng.wait_ge(exp_ok, b + 1)
                e3 = ex[:, b, :].rearrange("p (n q) -> p n q", q=NP)
                link(V.tensor_reduce(sm[:, b, :], e3, AX.X, ALU.add))
                link(V.reciprocal(sm[:, b, :], sm[:, b, :]))
                link(V.tensor_tensor(wt[:, b, :].rearrange("p (n q) -> p n q", q=NP), e3,
                                     sm[:, b, :].unsqueeze(2).to_broadcast([P, T * NHD, NP]), ALU.mult))

            def indices(b):
                t = slice(b * T, (b + 1) * T)
                off = pr[:, t, 0:HP]
                link(V.tensor_scalar(cc[:, :, :], off, C + 1.0, -C - 1.0, ALU.min, ALU.max))
                link(V.scalar_tensor_tensor(out=ia[:, :, :], in0=cc[:, :, :], scalar=-1.0, in1=cc[:, :, :],
                                            op0=ALU.mult, op1=ALU.max))
                V.tensor_scalar(ng[:, :, :], off, 0.0, None, ALU.is_lt)
                link(V.tensor_copy(ii[:, :, :], ia[:, :, :]))
                link(V.tensor_tensor(ig[:, :, :], ii[:, :, :], ia[:, :, :], ALU.is_gt))
                link(V.tensor_tensor(fl[:, :, :], ii[:, :, :], ig[:, :, :], ALU.subtract))
                V.scalar_tensor_tensor(out=ng[:, :, :], in0=fl[:, :, :], scalar=0.0, in1=ng[:, :, :],
                                       op0=ALU.is_gt, op1=ALU.mult)
                link(V.tensor_scalar(cc[:, :, :], fl[:, :, :], -2.0, float(C), ALU.mult, ALU.add))
                link(V.tensor_tensor(cc[:, :, :], cc[:, :, :], ng[:, :, :], ALU.mult))
                link(V.tensor_tensor(cc[:, :, :], cc[:, :, :], fl[:, :, :], ALU.add))
                link(V.tensor_scalar(ix[:, :, :], cc[:, :, :], 0.0, C - 1.0, ALU.max, ALU.min))
                link(V.tensor_scalar(ih[:, :, :], ix[:, :, :], 4, None, ALU.arith_shift_right))
                V.tensor_copy(lh[:, t, HP:2 * HP], ih[:, :, :])
                V.scalar_tensor_tensor(out=lh[:, t, 0:HP], in0=ih[:, :, :], scalar=-float(LO), in1=ix[:, :, :],
                                       op0=ALU.mult, op1=ALU.add).then_inc(lh_ok, 1)

            def table_in(b):
                eng.wait_ge(xnT_ok, b + 1)
                V.tensor_scalar(tv[:, b, :], own_hi[:, :], xnT[:, b, 0:1], None, ALU.mult).then_inc(tv_ok, 1)

            def table_out(b):
                eng.wait_ge(tp_ok, b + 1)
                link(V.tensor_copy(tr[:, 0, :], ps_w[:, b * HI:(b + 1) * HI]))
                link(V.tensor_copy(t3[:, 0, :], tr[:, 0, :]))
                link(V.tensor_tensor(tr[:, 1, :], tr[:, 0, :], t3[:, 0, :], ALU.subtract))
                link(V.tensor_copy(t3[:, 1, :], tr[:, 1, :]))
                link(V.tensor_tensor(t3[:, 2, :], tr[:, 1, :], t3[:, 1, :], ALU.subtract))
                V.tensor_tensor(tbd[:, b, :, :, :],
                                own_hi[:, :].unsqueeze(1).unsqueeze(3).to_broadcast([P, PIECES, JL, HI]),
                                t3[:, :, :].unsqueeze(2).to_broadcast([P, PIECES, JL, HI]), ALU.mult
                                ).then_inc(tbd_ok, 1)

            def onehot(b):
                eng.wait_ge(ld_rep[b], 16 * (QL + QH))
                if b >= 1:
                    eng.wait_ge(look_ok, 2 * b)
                V.tensor_scalar(oh[:, :, :], rep_lo[:, b, :, :], col[:, 0:1], None, ALU.is_equal).then_inc(oh_ok, 1)

            def pick(b, q):
                eng.wait_ge(look_ok, 2 * b + q + 1)
                if b >= 1 and q == 0:
                    eng.wait_ge(got_ok, b)
                V.scalar_tensor_tensor(out=ar[:, q, :], in0=rep_hi[:, b, q, :], scalar=col[:, 1:2],
                                       in1=(ps_b if q == 0 else ps_a)[:, :], op0=ALU.is_equal, op1=ALU.mult
                                       ).then_inc(pick_ok, 1)

            def attend(b):
                t = slice(b * T, (b + 1) * T)
                eng.wait_ge(got_ok, b + 1)
                V.tensor_tensor(gw[:, :, :], ps_b[:, 0:T * HP].rearrange("p (t n) -> p t n", t=T),
                                wt[:, b, :].rearrange("p (t n) -> p t n", t=T), ALU.mult).then_inc(gw_ok, 1)
                eng.wait_ge(gw_ok, b + 1)
                link(V.tensor_reduce(ss[:, t], gw[:, :, :], AX.X, ALU.add))
                if b == 0:
                    eng.wait_ge(cwp_ok, 1)
                    V.tensor_copy(cw[:, :], ps_y[:, 0:C]).then_inc(cw_ok, 1)
                    eng.wait_ge(cw_ok, 1)
                eng.wait_ge(xb_ok, b + 1)
                for u in range(b * T, (b + 1) * T):
                    ins = V.scalar_tensor_tensor(out=x2[:, u, :], in0=cw[:, :], scalar=ss[:, u:u + 1],
                                                 in1=xb[:, u, :], op0=ALU.mult, op1=ALU.add)
                link(ins)

            def x_lo(b):
                eng.wait_ge(xhi_ok, b + 1)
                if b >= 2:
                    eng.wait_ge(pu_ok, M * (b - 1))
                V.tensor_tensor(xlo[:, b % 2, :], ps_a[:, :], xhi[:, b % 2, :].bitcast(fp32), ALU.subtract
                                ).then_inc(xlo_ok, 1)

            def top2(b):
                eng.wait_ge(scp_ok, b + 1)
                V.tensor_copy(sc[:, :, :], ps_a[:, 0:T * NE].rearrange("p (t e) -> p t e", t=T)).then_inc(sc_ok, 1)
                eng.wait_ge(sc_ok, b + 1)

                def wide(v):
                    return v.unsqueeze(2).to_broadcast([P, T, NE])

                rank3 = rank[:, :].unsqueeze(1).to_broadcast([P, T, NE])

                def first_max(s, top, one, spare):
                    link(V.tensor_reduce(tm[:, top, :], s, AX.X, ALU.max))
                    link(V.tensor_tensor(tk[:, spare, :, :], s, wide(tm[:, top, :]), ALU.is_equal))
                    link(V.tensor_tensor(tk[:, spare, :, :], tk[:, spare, :, :], rank3, ALU.mult))
                    link(V.tensor_reduce(tm[:, 4, :], tk[:, spare, :, :], AX.X, ALU.max))
                    link(V.tensor_tensor(tk[:, one, :, :], rank3, wide(tm[:, 4, :]), ALU.is_equal))

                first_max(sc[:, :, :], 0, 0, 2)
                link(V.scalar_tensor_tensor(out=tk[:, 3, :, :], in0=tk[:, 0, :, :], scalar=LOWEST, in1=sc[:, :, :],
                                            op0=ALU.mult, op1=ALU.add))
                first_max(tk[:, 3, :, :], 1, 1, 2)
                V.tensor_tensor(tm[:, 5, :], tm[:, 0, :], tm[:, 1, :], ALU.subtract).then_inc(gap_ok, 1)

            def gates(b):
                def wide(v):
                    return v.unsqueeze(2).to_broadcast([P, T, NE])

                eng.wait_ge(th_ok, b + 1)
                V.tensor_scalar(tm[:, 2, :], tm[:, 6, :], 0.5, 0.5, ALU.mult, ALU.add)
                link(V.tensor_scalar(tm[:, 3, :], tm[:, 6, :], -0.5, 0.5, ALU.mult, ALU.add))
                V.tensor_tensor(tk[:, 4, :, :], tk[:, 0, :, :], wide(tm[:, 2, :]), ALU.mult)
                link(V.tensor_tensor(tk[:, 5, :, :], tk[:, 1, :, :], wide(tm[:, 3, :]), ALU.mult))
                link(V.tensor_tensor(tk[:, 6, :, :], tk[:, 4, :, :], tk[:, 5, :, :], ALU.add))
                if b >= 1:
                    eng.wait_ge(gTp_ok, b)
                link(V.tensor_copy(g3[:, :, 0, :], tk[:, 6, :, :]))
                link(V.tensor_tensor(tk[:, 7, :, :], tk[:, 6, :, :], g3[:, :, 0, :], ALU.subtract))
                link(V.tensor_copy(g3[:, :, 1, :], tk[:, 7, :, :]))
                V.tensor_tensor(g3[:, :, 2, :], tk[:, 7, :, :], g3[:, :, 1, :], ALU.subtract).then_inc(g3_ok, 1)

            def front(b):
                eng.wait_ge(ld_x[b], 16)
                stats(xs, st6, mv, b, var_ok)
                normalise(xn, xs, mv, rs, b, rs_ok, xn_ok)
                table_in(b)
                project(b)
                indices(b)
                weights_in(b)
                table_out(b)
                weights_out(b)

            front(0)
            split_gate()
            onehot(0)
            pick(0, 0)
            pick(0, 1)
            attend(0)
            stats(x2, st6b, mvb, 0, varb_ok)
            front(1)
            normalise(xn2, x2, mvb, rsb, 0, rsb_ok, xn2_ok)
            x_lo(0)
            front(2)
            top2(0)
            gates(0)
            front(3)

            def emit(b):
                t = slice(b * T, (b + 1) * T)
                eng.wait_ge(yp_ok, b + 1)
                V.tensor_tensor(yo[:, t, :], ps_a[:, :].rearrange("p (t c) -> p t c", t=T), x2[:, t, :], ALU.add
                                ).then_inc(out_ok, 1)

            for b in range(B):
                for m in range(M):
                    k = b * M + m
                    eng.wait_ge(sg_ok, k + 1)
                    eng.wait_ge(pu_ok, k + 1)
                    V.tensor_tensor(su[:, k % 2, :], sg[:, k % 2, :], ps_u[k % 2][:, :], ALU.mult).then_inc(su_ok, 1)
                    eng.wait_ge(pw_ok, k + 1)
                    eng.wait_ge(su_ok, k + 1)
                    if k >= NH:
                        eng.wait_ge(hlo_ok, k - NH + 1)
                    V.tensor_tensor(hh[:, k % NH, :], su[:, k % 2, :], ps_w[:, :], ALU.mult).then_inc(hh_ok, 1)
                    if m == 2 and b >= 1:
                        emit(b - 1)
                    if b + 1 < B:
                        if m == 0:
                            onehot(b + 1)
                        if m == 2:
                            pick(b + 1, 0)
                        if m == 3:
                            pick(b + 1, 1)
                        if m == 4:
                            attend(b + 1)
                        if m == 5:
                            stats(x2, st6b, mvb, b + 1, varb_ok)
                        if m == 6:
                            eng.wait_ge(xn2p_ok, b + 1)
                            normalise(xn2, x2, mvb, rsb, b + 1, rsb_ok, xn2_ok)
                        if m == 7:
                            x_lo(b + 1)
                        if m == 8:
                            top2(b + 1)
                        if m == 9:
                            gates(b + 1)
            emit(B - 1)

        @block.tensor
        def _(pe):
            def mm(o, l, r, start=True, stop=True):
                return nc.tensor.matmul(o, l, r, start=start, stop=stop)

            def front(b):
                pe.wait_ge(xn_ok, b + 1)
                if b >= 2:
                    pe.wait_ge(xnT_ok, b - 1)
                for t in range(T):
                    last = nc.tensor.transpose(ps_g[b % 2][:, t * P:(t + 1) * P], xn[:, b * T + t, :], ident[:, :])
                last.then_inc(xnp_ok, 1)
                pe.wait_ge(xnT_ok, b + 1)
                if b >= 2:
                    pe.wait_ge(pr_ok, b - 1)
                for t in range(T):
                    last = mm(ps_u[b % 2][:, t * 2 * HP:(t + 1) * 2 * HP], xnT[:, b, t * P:(t + 1) * P], wcat[:, :])
                last.then_inc(prp_ok, 1)
                pe.wait_ge(tv_ok, b + 1)
                mm(ps_w[:, b * HI:(b + 1) * HI], sel_lo[:, :], tv[:, b, :]).then_inc(tp_ok, 1)
                pe.wait_ge(lh_ok, b + 1)
                if b >= 2:
                    pe.wait_ge(lhT_ok, b - 1)
                for t in range(T):
                    last = nc.tensor.transpose(ps_u[b % 2][0:2 * HP, 256 + t * 64:256 + (t + 1) * 64].bitcast(bf16),
                                               lh[:, b * T + t, :], identb[:, :])
                last.then_inc(lhp_ok, 1)

            def look(b, half):
                bank_ = ps_b if half == 0 else ps_a
                if half == 0:
                    pe.wait_ge(oh_ok, b + 1)
                    pe.wait_ge(tbd_ok, b + 1)
                    if b >= 1:
                        pe.wait_ge(gT_ok, b)
                elif b >= 2:
                    pe.wait_ge(out_ok, b - 1)
                elif b == 1:
                    pe.wait_ge(sc_ok, 1)
                for r in range(2):
                    q = 2 * half + r
                    for i in range(PIECES):
                        last = mm(bank_[64 * r:64 * r + 64, :], tbd[:, b, i, :, :].rearrange("p j a -> p (j a)"),
                                  oh[:, q, :], start=(i == 0), stop=(i == PIECES - 1))
                last.then_inc(look_ok, 1)

            def collect(b):
                pe.wait_ge(pick_ok, 2 * b + 2)
                for t in range(T):
                    for q in range(QH):
                        last = mm(ps_b[:, t * HP + q * JH:t * HP + (q + 1) * JH], ar[:, q, t * P:(t + 1) * P],
                                  sum_hi[:, :])
                last.then_inc(got_ok, 1)

            def turn_x(b):
                pe.wait_ge(xn2_ok, b + 1)
                for t in range(T):
                    last = nc.tensor.transpose(ps_a[:, t * P:(t + 1) * P], xn2[:, t, :], ident[:, :])
                last.then_inc(xn2p_ok, 1)

            def scores(b):
                pe.wait_ge(xhi_ok, b + 1)
                pe.wait_ge(xlo_ok, b + 1)
                for t in range(T):
                    terms = [(xhi, wgt_hi), (xhi, wgt_lo), (xlo, wgt_hi), (xlo, wgt_lo)]
                    for i, (a, w) in enumerate(terms):
                        last = mm(ps_a[:, t * NE:(t + 1) * NE], a[:, b % 2, t * P:(t + 1) * P], w[:, :],
                                  start=(i == 0), stop=(i == len(terms) - 1))
                last.then_inc(scp_ok, 1)

            def turn_g(b):
                pe.wait_ge(g3_ok, b + 1)
                pe.wait_ge(gw_ok, b + 1)
                for t in range(T):
                    last = nc.tensor.transpose(ps_b[0:GK, t * 64:(t + 1) * 64].bitcast(bf16),
                                               g3[:, t, :, :].rearrange("p k e -> p (k e)"), identb[:, :])
                last.then_inc(gTp_ok, 1)

            pe.wait_ge(pool_c, 7)
            pe.wait_ge(wcat_ok, 2)
            pe.wait_ge(ld_o, 48)
            mm(ps_y[:, 0:C], ones[:, :], wo[:, :]).then_inc(cwp_ok, 1)
            pe.wait_ge(dve_c, 1)
            front(0)
            look(0, 0)
            look(0, 1)
            collect(0)
            front(1)
            turn_x(0)
            pe.wait_ge(wgt_ok, 2)
            scores(0)
            front(2)
            turn_g(0)
            front(3)
            pe.wait_ge(exp_ok, B)

            def down(j):
                c = j % M
                pe.wait_ge(hhi_ok, j + 1)
                pe.wait_ge(hlo_ok, j + 1)
                if c == 0 and j > 0:
                    pe.wait_ge(y_ok, j // M)
                wh, wl = (w[:, 2, c * P:(c + 1) * P] for w in (whi, wlo))
                mm(ps_y[:, :], wh, hhi[:, j % NH, :], start=(c == 0), stop=False)
                mm(ps_y[:, :], wl, hhi[:, j % NH, :], start=False, stop=False)
                mm(ps_y[:, :], wh, hlo[:, j % NH, :], start=False, stop=(c == M - 1)).then_inc(dn_ok, 1)

            for b in range(B):
                for m in range(M):
                    k = b * M + m
                    xh, xl = xhi[:, b % 2, :], xlo[:, b % 2, :]
                    cols = slice(m * P, (m + 1) * P)
                    for i, (ps, ok, free) in enumerate([(ps_g, pg_ok, sg_ok), (ps_u, pu_ok, su_ok)]):
                        if k >= 2:
                            pe.wait_ge(free, k - 1)
                        elif k == 0:
                            pe.wait_ge(wlo_ok, i + 1)
                            pe.wait_ge(lhT_ok, B)
                            pe.wait_ge(pr_ok, B)
                            pe.wait_ge(tbd_ok, B)
                        mm(ps[k % 2][:, :], whi[:, i, cols], xh, start=True, stop=False)
                        mm(ps[k % 2][:, :], wlo[:, i, cols], xh, start=False, stop=False)
                        mm(ps[k % 2][:, :], whi[:, i, cols], xl, start=False, stop=True).then_inc(ok, 1)
                    if k == LAG:
                        pe.wait_ge(wlo_ok, 3)
                        pe.wait_ge(cw_ok, 1)
                    if k >= LAG:
                        down(k - LAG)
                    if m == 0:
                        pe.wait_ge(gT_ok, b + 1)
                    if k >= 1:
                        pe.wait_ge(hh_ok, k)
                    mm(ps_w[:, :], spread[:, cols], gT[:, b % 2, :]).then_inc(pw_ok, 1)
                    if m == 2 and b >= 1:
                        pe.wait_ge(y_ok, b)
                        for t in range(T):
                            last = nc.tensor.transpose(ps_a[:, t * P:(t + 1) * P], ys[:, t * P:(t + 1) * P],
                                                       ident[:, :])
                        last.then_inc(yp_ok, 1)
                    if b + 1 < B:
                        if m == 1:
                            look(b + 1, 0)
                        if m == 3:
                            look(b + 1, 1)
                        if m == 4:
                            collect(b + 1)
                        if m == 7:
                            turn_x(b + 1)
                        if m == 8:
                            scores(b + 1)
                        if m == 10:
                            turn_g(b + 1)
            for j in range(B * M - LAG, B * M):
                down(j)
            pe.wait_ge(y_ok, B)
            for t in range(T):
                last = nc.tensor.transpose(ps_a[:, t * P:(t + 1) * P], ys[:, t * P:(t + 1) * P], ident[:, :])
            last.then_inc(yp_ok, 1)


_INS = ['L0_attn_x', 'L0_attn_W_off', 'L0_attn_b_off', 'L0_attn_W_attn', 'L0_attn_b_attn', 'L0_attn_W_out',
        'L0_attn_b_out', 'L0_ffn_w_gate', 'L0_ffn_w_g', 'L0_ffn_w_u', 'L0_ffn_w_d']


def kernel(**inputs):
    import numpy as _np
    import concourse.bacc as _bacc
    from concourse import mybir as _mybir
    from concourse.bass_utils import run_bass_kernel_spmd as _run

    nc = _bacc.Bacc("TRN2", target_bir_lowering=False, num_devices=1)
    arrays, args = {}, []
    for name in _INS:
        a = _np.ascontiguousarray(inputs[name])
        arrays[f"in_{name}_dram"] = a
        args.append(nc.dram_tensor(f"in_{name}_dram", a.shape, _mybir.dt.from_np(a.dtype), kind="ExternalInput").ap())
    shape = arrays[f"in_{_INS[0]}_dram"].shape
    args.append(nc.dram_tensor("out_0_dram", shape, _mybir.dt.float32, kind="ExternalOutput").ap())
    deform_attn_then_moe(nc, *args)
    r = _run(nc, [arrays], core_ids=[0])
    return r.results[0]["out_0_dram"]
```

```python
import concourse.bass as bass
from concourse import mybir
from contextlib import ExitStack


def deform_attn_then_moe(nc, x, w_off, b_off, w_attn, b_attn, w_out, b_out, w_gate, w_g, w_u, w_d, out):
    fp32, fp32r, bf16, i32 = (mybir.dt.float32, mybir.dt.float32r, mybir.dt.bfloat16, mybir.dt.int32)
    ALU = mybir.AluOpType
    ACT = mybir.ActivationFunctionType
    AX = mybir.AxisListType

    B, N, C = x.shape
    P = 128
    T = N // P
    NE, _, FM = w_g.shape
    HALL = NE * FM
    M = HALL // P
    HP = w_attn.shape[1]
    NP = 4
    NHD = HP // NP
    LO, HI = 16, C // 16
    JL = P // LO
    QL = HP // JL
    PIECES = 3
    GK = 2 * NE
    EPS = 1e-5
    LOWEST = -3.0e38
    LAG = 3
    NH = 3
    NS = 4

    w_g_v = w_g.rearrange("e d m -> d e m")
    w_u_v = w_u.rearrange("e d m -> d e m")
    w_d_v = w_d.rearrange("e m d -> (e m) d").rearrange("(c p) d -> p c d", p=P)

    ctx = ExitStack()
    with ctx:
        def sb(name, shape, dt=fp32):
            return ctx.enter_context(nc.sbuf_tensor(name, shape, dt))

        def sem(name):
            return ctx.enter_context(nc.semaphore(name))

        xs = sb("xs", [P, B * T, C])
        xb = sb("xb", [P, B * T, C])
        x2 = sb("x2", [P, B * T, C])
        wp = sb("wp", [P, 3 * HP])
        bp = sb("bp", [P, 3 * HP])
        wcat = sb("wcat", [P, 2 * HP])
        bcat = sb("bcat", [P, 2 * HP])
        wo = sb("wo", [P, C])
        bo = sb("bo", [P, C])
        cw = sb("cw", [P, C])
        wgt = sb("wgt", [P, NE])
        wgt2 = sb("wgt2", [P, 2, NE], fp32r)
        raw = sb("raw", [P, 3, HALL])
        whi = sb("whi", [P, 3, HALL], fp32r)
        wlo = sb("wlo", [P, 3, HALL], fp32r)
        ones = sb("ones", [P, P])
        ident = sb("ident", [P, P])
        identb = sb("identb", [P, P], bf16)
        part = sb("part", [P, 1], i32)
        bits = sb("bits", [P, 4], i32)
        col = sb("col", [P, 4])
        row_n = sb("row_n", [P, HP], i32)
        seat = sb("seat", [HP, QL * JL, LO], bf16)
        row_hi_i = sb("row_hi_i", [P, HI, JL], i32)
        row_hi = sb("row_hi", [P, HI, JL], bf16)
        rank_i = sb("rank_i", [P, NE], i32)
        rank = sb("rank", [P, NE])
        sel_lo = sb("sel_lo", [P, P])
        own = sb("own", [P, HI])
        spread = sb("spread", [GK, HALL], fp32r)
        mhalf = sb("mhalf", [P, B * T])
        st6 = sb("st6", [P, B * T, 6])
        mv = sb("mv", [P, B * T, 2])
        ve = sb("ve", [P, B * T])
        rs = sb("rs", [P, B * T])
        nb = sb("nb", [P, B * T])
        warm = sb("warm", [P, 1])
        xn = sb("xn", [P, 2 * T, C])
        xnT = sb("xnT", [P, B, N])
        pr = sb("pr", [P, B * T, 2 * HP])
        mx = sb("mx", [P, B * T, NHD])
        ex = sb("ex", [P, B * T, NHD, NP])
        sm = sb("sm", [P, B * T, NHD])
        wt = sb("wt", [P, B * T, HP])
        ia = sb("ia", [P, B * T, HP])
        ii = sb("ii", [P, B * T, HP], i32)
        ig = sb("ig", [P, B * T, HP])
        fl = sb("fl", [P, B * T, HP])
        ng = sb("ng", [P, B * T, HP])
        cc = sb("cc", [P, B * T, HP])
        ix = sb("ix", [P, B * T, HP], i32)
        ih = sb("ih", [P, B * T, HP], i32)
        lo = sb("lo", [P, B * T, HP], bf16)
        hi = sb("hi", [P, B * T, HP], bf16)
        tv = sb("tv", [P, B, HI])
        t3 = sb("t3", [P, B, PIECES, HI], bf16)
        tr = sb("tr", [P, B, 2, HI])
        tbd = sb("tbd", [P, B, PIECES, HI, JL], bf16)
        loT = sb("loT", [HP, N], bf16)
        rep = sb("rep", [P, QL, N], bf16)
        oh = sb("oh", [P, QL, N], bf16)
        eqh = sb("eqh", [P, T * QL, HI, JL], bf16)
        aw = sb("aw", [P, T * QL, HI, JL])
        junk = sb("junk", [P, T, QL * HI * JL])
        ss = sb("ss", [P, B * T])
        st6b = sb("st6b", [P, B * T, 6])
        mvb = sb("mvb", [P, B * T, 2])
        veb = sb("veb", [P, B * T])
        rsb = sb("rsb", [P, B * T])
        xn2 = sb("xn2", [P, T, C])
        xhi = sb("xhi", [P, 2, N], fp32r)
        xlo = sb("xlo", [P, 2, N], fp32r)
        sc = sb("sc", [P, T, NE])
        top = sb("top", [P, T, 8])
        tkey = sb("tkey", [P, T, 8])
        kgt = sb("kgt", [P, T, NE])
        keq = sb("keq", [P, T, NE])
        key = sb("key", [P, T, NE])
        one1 = sb("one1", [P, T, NE])
        both = sb("both", [P, T, NE])
        sign = sb("sign", [P, T, NE])
        gap = sb("gap", [P, T])
        th = sb("th", [P, T])
        gs = sb("gs", [P, T, NE])
        g2 = sb("g2", [P, T, 2, NE], fp32r)
        gT = sb("gT", [GK, 2, N], fp32r)
        sg = sb("sg", [P, 2, N])
        su = sb("su", [P, NH, N])
        hh = sb("hh", [P, NH, N])
        hhi = sb("hhi", [P, NS, N], fp32r)
        hlo = sb("hlo", [P, NS, N], fp32r)
        gw = sb("gw", [P, 2, N])
        ys = sb("ys", [P, N])

        def bank(name):
            return ctx.enter_context(nc.psum_tensor(name, [P, 512], fp32))

        ps_g = [bank("ps_g0"), bank("ps_g1")]
        ps_u = [bank("ps_u0"), bank("ps_u1")]
        ps_w, ps_y = bank("ps_w"), bank("ps_y")
        ps_s = [bank("ps_s0"), bank("ps_s1")]

        ld_x = [sem(f"ld_x{b}") for b in range(B)]
        ld_p, ld_wo, ld_bo, ld_wgt = map(sem, ["ld_p", "ld_wo", "ld_bo", "ld_wgt"])
        ld_w = [sem(f"ld_w{i}") for i in range(3)]
        st_out = sem("st_out")
        pool_c, ident_ok, identb_ok, sel_ok, seat_ok, spread_ok, wcat_ok, whi_ok, wlo_ok, cwp_ok, cw_ok, wgt_ok = map(
            sem, ["pool_c", "ident_ok", "identb_ok", "sel_ok", "seat_ok", "spread_ok", "wcat_ok", "whi_ok", "wlo_ok",
                  "cwp_ok", "cw_ok", "wgt_ok"])
        dve, pool = sem("dve"), sem("pool")
        (var_ok, rs_ok, nb_ok, pr_ok, sub_ok, exp_ok, tv_ok, tp_ok, tr_ok, tbd_ok, lo_ok, wt_ok) = map(sem, [
            "var_ok", "rs_ok", "nb_ok", "pr_ok", "sub_ok", "exp_ok", "tv_ok", "tp_ok", "tr_ok", "tbd_ok", "lo_ok", "wt_ok"])
        (hi_ok, xn_ok, xnp_ok, xnT_ok, prp_ok, xb_ok, eqh_ok, aw_ok, oh_ok, look_ok, ss_ok) = map(sem, [
            "hi_ok", "xn_ok", "xnp_ok", "xnT_ok", "prp_ok", "xb_ok", "eqh_ok", "aw_ok", "oh_ok", "look_ok", "ss_ok"])
        lop_ok, loT_ok = sem("lop_ok"), sem("loT_ok")
        repp_ok, rep_ok = sem("repp_ok"), sem("rep_ok")
        (varb_ok, rsb_ok, xn2_ok, xn2p_ok, xhi_ok, xlo_ok, scp_ok, sc_ok, gap_ok, th_ok, g2_ok, gTp_ok,
         gT_ok, y_ok, yp_ok, out_ok) = map(sem, [
             "varb_ok", "rsb_ok", "xn2_ok", "xn2p_ok", "xhi_ok", "xlo_ok", "scp_ok", "sc_ok", "gap_ok",
             "th_ok", "g2_ok", "gTp_ok", "gT_ok", "y_ok", "yp_ok", "out_ok"])
        (pg_ok, pu_ok, pw_ok, gw_ok, sg_ok, su_ok, hh_ok, hhi_ok, hlo_ok, dn_ok) = map(sem, [
            "pg_ok", "pu_ok", "pw_ok", "gw_ok", "sg_ok", "su_ok", "hh_ok", "hhi_ok", "hlo_ok", "dn_ok"])

        TURNS = [(0, 1), (1, 2), (2, B)]
        PR_AT = {0: (ps_u[0], 0), 1: (ps_u[1], 0), 2: (ps_y, 0), 3: (ps_y, 256)}

        DIGITS_AT = {b: ps_s for b in range(B)}
        DIGITS_AT[1] = ps_u

        def turn(b):
            return next(i for i, (b0, b1) in enumerate(TURNS) if b < b1)

        def tiles(b0, b1):
            return slice(b0 * T, b1 * T)

        block = ctx.enter_context(nc.Block())

        @block.sync
        def _(sp):
            xv = x.rearrange("b (t p) c -> b p t c", p=P)
            sp.dma_start(xs[:, 0:T, :], xv[0]).then_inc(ld_x[0], 16)
            sp.dma_start(wp[:, 0:2 * HP], w_off).then_inc(ld_p, 16)
            sp.dma_start(wp[:, 2 * HP:3 * HP], w_attn).then_inc(ld_p, 16)
            for b in range(1, B):
                sp.dma_start(xs[:, b * T:(b + 1) * T, :], xv[b]).then_inc(ld_x[b], 16)
            sp.dma_start(raw[:, 0, :].rearrange("p (e m) -> p e m", e=NE), w_g_v).then_inc(ld_w[0], 16)
            sp.dma_start(raw[:, 1, :].rearrange("p (e m) -> p e m", e=NE), w_u_v).then_inc(ld_w[1], 16)
            sp.dma_start(raw[:, 2, :].rearrange("p (c d) -> p c d", c=M), w_d_v).then_inc(ld_w[2], 16)
            ov = out.rearrange("b (t p) c -> b p t c", p=P)
            for b in range(B):
                sp.wait_ge(out_ok, b + 1)
                sp.dma_start(ov[b], x2[:, b * T:(b + 1) * T, :]).then_inc(st_out, 16)
            sp.wait_ge(st_out, 16 * B)

        @block.gpsimd
        def _(eng):
            n = [0]

            def link(ins):
                n[0] += 1
                ins.then_inc(pool, 1)
                eng.wait_ge(pool, n[0])

            link(eng.memset(ident[:, :], 0.0))
            eng.affine_select(out=ident[:, :], in_=ident[:, :], compare_op=ALU.not_equal, fill=1.0, base=0,
                              pattern=[[-1, P]], channel_multiplier=1).then_inc(ident_ok, 1)
            eng.iota(part[:, :], pattern=[[0, 1]], base=0, channel_multiplier=1).then_inc(pool_c, 1)
            eng.iota(row_n[:, :], pattern=[[1, HP]], base=0, channel_multiplier=0).then_inc(pool_c, 1)
            eng.iota(row_hi_i[:, :, :], pattern=[[1, HI], [0, JL]], base=0, channel_multiplier=0).then_inc(pool_c, 1)
            eng.iota(rank_i[:, :], pattern=[[-1, NE]], base=NE, channel_multiplier=0).then_inc(pool_c, 1)
            eng.memset(ones[:, :], 1.0).then_inc(pool_c, 1)
            link(eng.memset(mhalf[:, :], -0.5))

            def rstd(v, m, r, t, ready, count, done):
                eng.wait_ge(ready, count)
                link(eng.tensor_scalar(v[:, t], m[:, t, 1], EPS, None, ALU.add))
                eng.tensor_tensor(r[:, t], v[:, t], mhalf[:, t], ALU.pow).then_inc(done, 1)

            def residual(b):
                t = tiles(b, b + 1)
                if b == 0:
                    eng.wait_ge(ld_bo, 16)
                eng.wait_ge(ld_x[b], 16)
                eng.tensor_tensor(xb[:, t, :], xs[:, t, :], bo[:, :].unsqueeze(1).to_broadcast([P, T, C]),
                                  ALU.add).then_inc(xb_ok, 1)

            def weights_lo(i):
                eng.wait_ge(whi_ok, i + 1)
                eng.tensor_tensor(wlo[:, i, :], raw[:, i, :], whi[:, i, :].bitcast(fp32), ALU.subtract
                                  ).then_inc(wlo_ok, 1)

            def weigh_hi(b):
                eng.wait_ge(eqh_ok, b + 1)
                eng.wait_ge(wt_ok, turn(b) + 1)
                if b >= 1:
                    eng.wait_ge(ss_ok, b)
                eng.tensor_tensor(aw[:, :, :, :], eqh[:, :, :, :],
                                  wt[:, tiles(b, b + 1), :].rearrange("p t (q j) -> p (t q) j", j=JL)
                                  .unsqueeze(2).to_broadcast([P, T * QL, HI, JL]), ALU.mult).then_inc(aw_ok, 1)

            rstd(ve, mv, rs, tiles(0, 1), var_ok, 1, rs_ok)
            residual(0)
            rstd(ve, mv, rs, tiles(1, 2), var_ok, 2, rs_ok)
            weights_lo(0)
            weigh_hi(0)
            rstd(ve, mv, rs, tiles(2, B), var_ok, 3, rs_ok)
            weights_lo(1)
            residual(1)
            rstd(veb, mvb, rsb, tiles(0, 1), varb_ok, 1, rsb_ok)
            weigh_hi(1)
            weights_lo(2)
            for b in range(B):
                for m in range(M):
                    k = b * M + m
                    eng.wait_ge(hhi_ok, k + 1)
                    if k >= NS:
                        eng.wait_ge(dn_ok, k - NS + 1)
                    eng.tensor_tensor(hlo[:, k % NS, :], hh[:, k % NH, :], hhi[:, k % NS, :].bitcast(fp32),
                                      ALU.subtract).then_inc(hlo_ok, 1)
                    if b + 1 < B:
                        if m == 3:
                            rstd(veb, mvb, rsb, tiles(b + 1, b + 2), varb_ok, b + 2, rsb_ok)
                    if b + 2 < B:
                        if m == 5:
                            residual(b + 2)
                        if m == 10:
                            weigh_hi(b + 2)

        @block.scalar
        def _(act):
            act.dma_start(bp[:, 0:2 * HP], b_off.partition_broadcast(P)).then_inc(ld_p, 16)
            act.dma_start(bp[:, 2 * HP:3 * HP], b_attn.partition_broadcast(P)).then_inc(ld_p, 16)
            act.dma_start(bo[:, :], b_out.partition_broadcast(P)).then_inc(ld_bo, 16)
            act.dma_start(wgt[:, :], w_gate).then_inc(ld_wgt, 16)
            act.dma_start(wo[:, :], w_out).then_inc(ld_wo, 16)
            A = nc.scalar.activation

            def channels(b):
                act.wait_ge(xnp_ok, b + 1)
                A(xnT[:, b, :], ps_g[b % 2][:, :], ACT.Copy).then_inc(xnT_ok, 1)

            def norm1(b):
                act.wait_ge(nb_ok, 1)
                act.wait_ge(xnp_ok, b - 1)
                for t in range(b * T, (b + 1) * T):
                    A(xn[:, t % (2 * T), :], xs[:, t, :], ACT.Identity, bias=nb[:, t:t + 1], scale=rs[:, t:t + 1]
                      ).then_inc(xn_ok, 1)

            def exps(i):
                t = tiles(*TURNS[i])
                act.wait_ge(sub_ok, i + 1)
                A(ex[:, t, :, :], ex[:, t, :, :], ACT.Exp).then_inc(exp_ok, 1)

            def weights_hi(i):
                act.wait_ge(ld_w[i], 16)
                A(whi[:, i, :], raw[:, i, :], ACT.Copy).then_inc(whi_ok, 1)

            def low_T(b):
                act.wait_ge(lop_ok, b + 1)
                if b >= 1:
                    act.wait_ge(repp_ok, QL * b)
                A(loT[:, :], DIGITS_AT[b][1][0:HP, 0:256].bitcast(bf16), ACT.Copy).then_inc(loT_ok, 1)

            def digits(b, q0, q1):
                for q in range(q0, q1):
                    act.wait_ge(repp_ok, b * QL + q + 1)
                    if b >= 1 and q == 0:
                        act.wait_ge(oh_ok, b)
                    A(rep[:, q, :], DIGITS_AT[b][q % 2][:, :], ACT.Copy).then_inc(rep_ok, 1)

            def x_hi(b):
                act.wait_ge(xn2p_ok, b + 1)
                if b >= 2:
                    act.wait_ge(pu_ok, M * (b - 1))
                A(xhi[:, b % 2, :], ps_s[0][:, :], ACT.Copy).then_inc(xhi_ok, 1)

            def split(b):
                act.wait_ge(gap_ok, b + 1)
                A(th[:, :], gap[:, :], ACT.Tanh, scale=0.5).then_inc(th_ok, 1)

            def gates_T(b):
                act.wait_ge(gTp_ok, b + 1)
                if b >= 2:
                    act.wait_ge(pw_ok, M * (b - 1))
                A(gT[:, b % 2, :], ps_s[1][0:GK, :], ACT.Copy).then_inc(gT_ok, 1)

            channels(0)
            weights_hi(0)
            channels(1)
            exps(0)
            low_T(0)
            digits(0, 0, QL)
            weights_hi(1)
            norm1(2)
            exps(1)
            channels(2)
            low_T(1)
            norm1(3)
            digits(1, 0, 2)
            channels(3)
            digits(1, 2, QL)
            x_hi(0)
            weights_hi(2)
            exps(2)
            act.wait_ge(ident_ok, 1)
            A(warm[:, :], ident[:, 0:1], ACT.Silu)
            split(0)

            def high(j):
                act.wait_ge(hh_ok, j + 1)
                if j >= NS:
                    act.wait_ge(dn_ok, j - NS + 1)
                A(hhi[:, j % NS, :], hh[:, j % NH, :], ACT.Copy).then_inc(hhi_ok, 1)

            def y_out(b):
                act.wait_ge(dn_ok, M * (b + 1))
                if b >= 1:
                    act.wait_ge(yp_ok, b)
                A(ys[:, :], ps_y[:, :], ACT.Copy).then_inc(y_ok, 1)

            def gate(j):
                act.wait_ge(pw_ok, j + 1)
                if j >= 2:
                    act.wait_ge(hh_ok, j - 1)
                A(gw[:, j % 2, :], ps_w[:, :], ACT.Copy).then_inc(gw_ok, 1)

            for b in range(B):
                for m in range(M):
                    k = b * M + m
                    act.wait_ge(pg_ok, k + 1)
                    if k >= 2:
                        act.wait_ge(su_ok, k - 1)
                    A(sg[:, k % 2, :], ps_g[k % 2][:, :], ACT.Silu).then_inc(sg_ok, 1)
                    if k == 1:
                        gates_T(0)
                    if k == 2:
                        gate(0)
                        gate(1)
                        high(0)
                    if k >= 2:
                        gate(k)
                        high(k - 1)
                    if m == 2 and b >= 1:
                        y_out(b - 1)
                    if b + 1 < B:
                        if m == 6:
                            x_hi(b + 1)
                        if m == 8:
                            split(b + 1)
                        if m == 10:
                            gates_T(b + 1)
                    if b + 2 < B:
                        if m == 7:
                            low_T(b + 2)
                        if m == 8:
                            digits(b + 2, 0, 2)
                        if m == 9:
                            digits(b + 2, 2, 4)
            high(B * M - 1)
            y_out(B - 1)

        @block.vector
        def _(eng):
            n = [0]
            V = nc.vector

            def did(ins):
                n[0] += 1
                ins.then_inc(dve, 1)
                return n[0]

            def after(step):
                eng.wait_ge(dve, step)

            def link(ins):
                after(did(ins))

            def stats(src, s6, m2, t0, t1):
                for t in range(t0, t1):
                    last = did(V.bn_stats(s6[:, t, :], src[:, t, :]))
                    if t > t0:
                        after(last - 2 if t > t0 + 1 else last - 1)
                        did(V.bn_aggr(m2[:, t - 1, :], s6[:, t - 1, :]))
                after(n[0] - 1)
                return V.bn_aggr(m2[:, t1 - 1, :], s6[:, t1 - 1, :])

            def normalise(dst, src, m2, r, b, done):
                for t in range(b * T, (b + 1) * T):
                    ins = V.tensor_scalar(dst[:, t % dst.shape[1], :], src[:, t, :], m2[:, t, 0:1], r[:, t:t + 1],
                                          ALU.subtract, ALU.mult)
                    ins.then_inc(done, 1)

            def neg_bias(t):
                eng.wait_ge(rs_ok, 3)
                V.scalar_tensor_tensor(out=nb[:, t], in0=mv[:, t, 0], scalar=-1.0, in1=rs[:, t],
                                       op0=ALU.mult, op1=ALU.mult).then_inc(nb_ok, 1)

            def norm1(b):
                eng.wait_ge(rs_ok, turn(b) + 1)
                if b >= 2:
                    eng.wait_ge(xnp_ok, b - 1)
                normalise(xn, xs, mv, rs, b, xn_ok)

            def norm2(b):
                eng.wait_ge(rsb_ok, b + 1)
                if b >= 1:
                    eng.wait_ge(xn2p_ok, b)
                normalise(xn2, x2, mvb, rsb, b, xn2_ok)

            def project(i):
                b0, b1 = TURNS[i]
                eng.wait_ge(prp_ok, b1)
                u, o = PR_AT[b0]
                nt = (b1 - b0) * T
                V.tensor_tensor(pr[:, tiles(b0, b1), :],
                                u[:, o:o + nt * 2 * HP].rearrange("p (t n) -> p t n", t=nt),
                                bcat[:, :].unsqueeze(1).to_broadcast([P, nt, 2 * HP]), ALU.add).then_inc(pr_ok, 1)
                eng.wait_ge(pr_ok, i + 1)

            step = {}

            def clamp(i):
                t = tiles(*TURNS[i])
                step["cc"] = did(V.tensor_scalar(cc[:, t, :], pr[:, t, 0:HP], C - 1.0, -float(C), ALU.min, ALU.max))

            def magnitude(i):
                t = tiles(*TURNS[i])
                after(step["cc"])
                step["ia"] = did(V.scalar_tensor_tensor(out=ia[:, t, :], in0=cc[:, t, :], scalar=-1.0,
                                                        in1=cc[:, t, :], op0=ALU.mult, op1=ALU.max))

            def to_int(i):
                t = tiles(*TURNS[i])
                after(step["ia"])
                step["ii"] = did(V.tensor_copy(ii[:, t, :], ia[:, t, :]))
                step["ng"] = did(V.tensor_scalar(ng[:, t, :], cc[:, t, :], -1.0, -float(C), ALU.is_le, ALU.mult))

            def rounded_up(i):
                t = tiles(*TURNS[i])
                after(step["ii"])
                step["ig"] = did(V.tensor_tensor(ig[:, t, :], ii[:, t, :], ia[:, t, :], ALU.is_gt))

            def wrap_by(i):
                t = tiles(*TURNS[i])
                after(step["ng"])
                step["fl"] = did(V.tensor_tensor(fl[:, t, :], ii[:, t, :], ng[:, t, :], ALU.add))

            def wrap(i):
                t = tiles(*TURNS[i])
                after(step["fl"])
                step["cc"] = did(V.tensor_tensor(cc[:, t, :], fl[:, t, :], ig[:, t, :], ALU.subtract))

            def index(i):
                t = tiles(*TURNS[i])
                after(step["cc"])
                step["ix"] = did(V.scalar_tensor_tensor(out=ix[:, t, :], in0=cc[:, t, :], scalar=-1.0,
                                                        in1=cc[:, t, :], op0=ALU.mult, op1=ALU.max))

            def high_digit(i):
                t = tiles(*TURNS[i])
                after(step["ix"])
                step["ih"] = did(V.tensor_scalar(ih[:, t, :], ix[:, t, :], 4, None, ALU.arith_shift_right))

            def both_digits(i):
                t = tiles(*TURNS[i])
                after(step["ih"])
                V.scalar_tensor_tensor(out=lo[:, t, :], in0=ih[:, t, :], scalar=-float(LO), in1=ix[:, t, :],
                                       op0=ALU.mult, op1=ALU.add).then_inc(lo_ok, 1)
                V.tensor_copy(hi[:, t, :], ih[:, t, :]).then_inc(hi_ok, 1)

            def logits(t):
                return pr[:, t, HP:2 * HP].rearrange("p t (h q) -> p t h q", q=NP)

            def points_max(i):
                t = tiles(*TURNS[i])
                step["mx"] = did(V.tensor_reduce(mx[:, t, :], logits(t), AX.X, ALU.max))

            def points_sub(i):
                t = tiles(*TURNS[i])
                after(step["mx"])
                nt = t.stop - t.start
                V.tensor_tensor(ex[:, t, :, :], logits(t), mx[:, t, :].unsqueeze(3).to_broadcast([P, nt, NHD, NP]),
                                ALU.subtract).then_inc(sub_ok, 1)

            def points_sum(i):
                t = tiles(*TURNS[i])
                eng.wait_ge(exp_ok, i + 1)
                step["sm"] = did(V.tensor_reduce(sm[:, t, :], ex[:, t, :, :], AX.X, ALU.add))

            def points_inv(i):
                t = tiles(*TURNS[i])
                after(step["sm"])
                step["sm"] = did(V.reciprocal(sm[:, t, :], sm[:, t, :]))

            def points_out(i):
                t = tiles(*TURNS[i])
                after(step["sm"])
                nt = t.stop - t.start
                V.tensor_tensor(wt[:, t, :].rearrange("p t (h q) -> p t h q", q=NP), ex[:, t, :, :],
                                sm[:, t, :].unsqueeze(3).to_broadcast([P, nt, NHD, NP]), ALU.mult
                                ).then_inc(wt_ok, 1)

            def table_in(i):
                b0, b1 = TURNS[i]
                eng.wait_ge(xnT_ok, b1)
                V.tensor_tensor(tv[:, b0:b1, :], own[:, :].unsqueeze(1).to_broadcast([P, b1 - b0, HI]),
                                xnT[:, b0:b1, 0:1].to_broadcast([P, b1 - b0, HI]), ALU.mult).then_inc(tv_ok, 1)

            def table_got(i):
                b0, b1 = TURNS[i]
                eng.wait_ge(tp_ok, i + 1)
                V.tensor_copy(tr[:, b0:b1, 0, :], ps_w[:, b0 * HI:b1 * HI].rearrange("p (b a) -> p b a", a=HI)
                              ).then_inc(tr_ok, 1)

            def table_1(i):
                b0, b1 = TURNS[i]
                eng.wait_ge(tr_ok, i + 1)
                step["t1"] = did(V.tensor_copy(t3[:, b0:b1, 0, :], tr[:, b0:b1, 0, :]))

            def table_rest(i):
                b0, b1 = TURNS[i]
                after(step["t1"])
                step["tr1"] = did(V.tensor_tensor(tr[:, b0:b1, 1, :], tr[:, b0:b1, 0, :], t3[:, b0:b1, 0, :],
                                                  ALU.subtract))

            def table_2(i):
                b0, b1 = TURNS[i]
                after(step["tr1"])
                step["t2"] = did(V.tensor_copy(t3[:, b0:b1, 1, :], tr[:, b0:b1, 1, :]))

            def table_3(i):
                b0, b1 = TURNS[i]
                after(step["t2"])
                step["t3"] = did(V.tensor_tensor(t3[:, b0:b1, 2, :], tr[:, b0:b1, 1, :], t3[:, b0:b1, 1, :],
                                                 ALU.subtract))

            def table_out(i):
                b0, b1 = TURNS[i]
                after(step["t3"])
                k = (b1 - b0) * PIECES
                V.tensor_tensor(tbd[:, b0:b1, :, :, :].rearrange("p b k a j -> p (b k) a j"),
                                own[:, :].unsqueeze(1).unsqueeze(1).to_broadcast([P, k, HI, JL]),
                                t3[:, b0:b1, :, :].rearrange("p b k a -> p (b k) a").unsqueeze(3)
                                .to_broadcast([P, k, HI, JL]), ALU.mult).then_inc(tbd_ok, 1)

            def hi_onehot(b):
                eng.wait_ge(hi_ok, turn(b) + 1)
                if b >= 1:
                    eng.wait_ge(aw_ok, b)
                V.tensor_tensor(eqh[:, :, :, :], row_hi[:, :, :].unsqueeze(1).to_broadcast([P, T * QL, HI, JL]),
                                hi[:, tiles(b, b + 1), :].rearrange("p t (q j) -> p (t q) j", j=JL)
                                .unsqueeze(2).to_broadcast([P, T * QL, HI, JL]), ALU.is_equal).then_inc(eqh_ok, 1)

            def lo_onehot(b):
                eng.wait_ge(rep_ok, QL * (b + 1))
                if b >= 1:
                    eng.wait_ge(look_ok, b * T // 2)
                V.tensor_scalar(oh[:, :, :], rep[:, :, :], col[:, 0:1], None, ALU.is_equal).then_inc(oh_ok, 1)

            def attend(b):
                eng.wait_ge(aw_ok, b + 1)
                w = QL * HI * JL
                for t in range(T):
                    if t % 2 == 0:
                        eng.wait_ge(look_ok, b * T // 2 + t // 2 + 1)
                    ins = V.tensor_tensor_reduce(junk[:, t, :], aw[:, t * QL:(t + 1) * QL, :, :]
                                                 .rearrange("p q a j -> p (q a j)"),
                                                 ps_s[t // 2][:, t % 2 * w:(t % 2 + 1) * w], 1.0, 0.0,
                                                 ALU.mult, ALU.add, ss[:, b * T + t:b * T + t + 1])
                ins.then_inc(ss_ok, 1)

            def add_attention(b):
                eng.wait_ge(ss_ok, b + 1)
                eng.wait_ge(xb_ok, b + 1)
                for u in range(b * T, (b + 1) * T):
                    ins = did(V.scalar_tensor_tensor(out=x2[:, u, :], in0=cw[:, :], scalar=ss[:, u:u + 1],
                                                     in1=xb[:, u, :], op0=ALU.mult, op1=ALU.add))
                step["x2"] = ins

            def stats2(b):
                after(step["x2"])
                stats(x2, st6b, mvb, b * T, (b + 1) * T).then_inc(varb_ok, 1)

            def x_lo(b):
                eng.wait_ge(xhi_ok, b + 1)
                if b >= 2:
                    eng.wait_ge(pu_ok, M * (b - 1))
                V.tensor_tensor(xlo[:, b % 2, :], ps_s[0][:, :], xhi[:, b % 2, :].bitcast(fp32), ALU.subtract
                                ).then_inc(xlo_ok, 1)

            def wide(v):
                return v.unsqueeze(2).to_broadcast([P, T, NE])

            def best(b):
                eng.wait_ge(scp_ok, b + 1)
                V.tensor_reduce(sc[:, :, :], ps_s[1][:, 0:T * 2 * NE].rearrange("p (t k e) -> p t e k", t=T, k=2),
                                AX.X, ALU.add).then_inc(sc_ok, 1)
                eng.wait_ge(sc_ok, b + 1)
                for t in range(T):
                    ins = V.max(top[:, t, :], sc[:, t, :])
                link(ins)
                V.tensor_tensor(gap[:, :], top[:, :, 0], top[:, :, 1], ALU.subtract).then_inc(gap_ok, 1)
                s1 = did(V.tensor_tensor(keq[:, :, :], sc[:, :, :], wide(top[:, :, 1]), ALU.is_equal))
                did(V.tensor_tensor(kgt[:, :, :], sc[:, :, :], wide(top[:, :, 1]), ALU.is_gt))
                after(s1)
                link(V.tensor_tensor(keq[:, :, :], keq[:, :, :], rank[:, :].unsqueeze(1).to_broadcast([P, T, NE]),
                                     ALU.mult))
                link(V.scalar_tensor_tensor(out=key[:, :, :], in0=kgt[:, :, :], scalar=2.0 * NE, in1=keq[:, :, :],
                                            op0=ALU.mult, op1=ALU.add))
                for t in range(T):
                    ins = V.max(tkey[:, t, :], key[:, t, :])
                link(ins)

            def chosen(b):
                did(V.tensor_tensor(both[:, :, :], key[:, :, :], wide(tkey[:, :, 1]), ALU.is_ge))
                link(V.tensor_tensor(one1[:, :, :], key[:, :, :], wide(tkey[:, :, 0]), ALU.is_ge))
                step["sign"] = did(V.scalar_tensor_tensor(out=sign[:, :, :], in0=one1[:, :, :], scalar=2.0,
                                                          in1=both[:, :, :], op0=ALU.mult, op1=ALU.subtract))

            def gates(b):
                eng.wait_ge(th_ok, b + 1)
                after(step["sign"])
                link(V.tensor_tensor(gs[:, :, :], sign[:, :, :], wide(th[:, :]), ALU.mult))
                link(V.tensor_tensor(gs[:, :, :], gs[:, :, :], both[:, :, :], ALU.add))
                if b >= 1:
                    eng.wait_ge(gTp_ok, b)
                link(V.tensor_scalar(g2[:, :, 0, :], gs[:, :, :], 0.5, None, ALU.mult))
                V.scalar_tensor_tensor(out=g2[:, :, 1, :], in0=gs[:, :, :], scalar=0.5,
                                       in1=g2[:, :, 0, :].bitcast(fp32), op0=ALU.mult, op1=ALU.subtract
                                       ).then_inc(g2_ok, 1)

            def stats1(b):
                eng.wait_ge(ld_x[b], 16)
                return stats(xs, st6, mv, b * T, (b + 1) * T)

            stats1(0).then_inc(var_ok, 1)
            eng.wait_ge(pool_c, 4)
            eng.wait_ge(ident_ok, 1)
            for i, (op, v) in enumerate([(ALU.bitwise_and, LO - 1), (ALU.bitwise_and, NE - 1),
                                         (ALU.arith_shift_right, 4), (ALU.arith_shift_right, 0)]):
                ins = V.tensor_scalar(bits[:, i:i + 1], part[:, :], v, None, op)
            cast = did(ins)
            did(V.tensor_copy(rank[:, :], rank_i[:, :]))
            did(V.tensor_copy(row_hi[:, :, :], row_hi_i[:, :, :]))
            after(cast)
            link(V.tensor_copy(col[:, :], bits[:, :]))
            eng.wait_ge(ld_p, 64)
            V.tensor_copy(wcat[:, 0:HP], wp[:, 0:2 * HP:2]).then_inc(wcat_ok, 1)
            V.tensor_copy(wcat[:, HP:2 * HP], wp[:, 2 * HP:3 * HP]).then_inc(wcat_ok, 1)
            norm1(0)
            stats1(1).then_inc(var_ok, 1)
            did(V.tensor_copy(bcat[:, 0:HP], bp[:, 0:2 * HP:2]))
            did(V.tensor_copy(bcat[:, HP:2 * HP], bp[:, 2 * HP:3 * HP]))
            link(V.tensor_scalar(own[:, :], row_hi_i[:, :, 0], col[:, 2:3], None, ALU.is_equal))
            V.tensor_scalar(sel_lo[:, :].rearrange("p (j b) -> p j b", b=LO),
                            row_n[:, 0:LO].unsqueeze(1).to_broadcast([P, JL, LO]), col[:, 0:1], None,
                            ALU.is_equal).then_inc(sel_ok, 1)
            table_in(0)
            norm1(1)
            project(0)
            clamp(0)
            points_max(0)
            magnitude(0)
            points_sub(0)
            to_int(0)
            table_got(0)
            rounded_up(0)
            table_1(0)
            wrap_by(0)
            V.tensor_copy(identb[:, :], ident[:, :]).then_inc(identb_ok, 1)
            wrap(0)
            table_rest(0)
            index(0)
            table_2(0)
            high_digit(0)
            table_3(0)
            both_digits(0)
            V.tensor_scalar(seat[:, :, :], row_n[0:HP, :].unsqueeze(2).to_broadcast([HP, QL * JL, LO]),
                            col[0:HP, 3:4], None, ALU.is_equal).then_inc(seat_ok, 1)
            points_sum(0)
            hi_onehot(0)
            V.tensor_scalar(spread[:, :].rearrange("k (e m) -> k e m", e=NE),
                            row_n[0:GK, 0:NE].unsqueeze(2).to_broadcast([GK, NE, FM]), col[0:GK, 1:2], None,
                            ALU.is_equal).then_inc(spread_ok, 1)
            points_inv(0)
            eng.wait_ge(ld_wgt, 16)
            table_out(0)
            points_out(0)
            did(stats1(2))
            stats1(3).then_inc(var_ok, 1)
            lo_onehot(0)
            project(1)
            clamp(1)
            points_max(1)
            magnitude(1)
            points_sub(1)
            to_int(1)
            neg_bias(tiles(2, B))
            rounded_up(1)
            table_in(1)
            wrap_by(1)
            V.tensor_copy(cw[:, :], ps_y[:, 0:C]).then_inc(cw_ok, 1)
            wrap(1)
            index(1)
            high_digit(1)
            both_digits(1)
            attend(0)
            eng.wait_ge(cw_ok, 1)
            add_attention(0)
            stats2(0)
            points_sum(1)
            table_got(1)
            hi_onehot(1)
            table_1(1)
            points_inv(1)
            points_out(1)
            norm2(0)
            table_rest(1)
            table_in(2)
            table_2(1)
            V.tensor_copy(wgt2[:, 0, :], wgt[:, :]).then_inc(wgt_ok, 1)
            table_3(1)
            eng.wait_ge(wgt_ok, 1)
            V.tensor_tensor(wgt2[:, 1, :], wgt[:, :], wgt2[:, 0, :].bitcast(fp32), ALU.subtract).then_inc(wgt_ok, 1)
            table_out(1)
            x_lo(0)
            lo_onehot(1)
            project(2)
            points_max(2)
            points_sub(2)
            best(0)
            chosen(0)
            table_got(2)

            def emit(b):
                t = tiles(b, b + 1)
                eng.wait_ge(yp_ok, b + 1)
                V.tensor_tensor(x2[:, t, :], ps_s[0][:, :].rearrange("p (t c) -> p t c", t=T), x2[:, t, :], ALU.add
                                ).then_inc(out_ok, 1)

            def up(k):
                eng.wait_ge(sg_ok, k + 1)
                eng.wait_ge(pu_ok, k + 1)
                V.tensor_tensor(su[:, k % NH, :], sg[:, k % 2, :], ps_u[k % 2][:, :], ALU.mult).then_inc(su_ok, 1)

            def gated(k):
                eng.wait_ge(su_ok, k + 1)
                eng.wait_ge(gw_ok, k + 1)
                if k >= NH:
                    eng.wait_ge(hlo_ok, k - NH + 1)
                V.tensor_tensor(hh[:, k % NH, :], su[:, k % NH, :], gw[:, k % 2, :], ALU.mult).then_inc(hh_ok, 1)

            for b in range(B):
                for m in range(M):
                    k = b * M + m
                    if k >= 3:
                        gated(k - 1)
                    up(k)
                    if k == 0:
                        gates(0)
                    if k == 1:
                        clamp(2)
                    if k == 2:
                        gated(0)
                        gated(1)
                    if b == 0:
                        if m == 1:
                            table_1(2)
                            magnitude(2)
                            table_rest(2)
                            to_int(2)
                        if m == 2:
                            rounded_up(2)
                            wrap_by(2)
                            table_2(2)
                        if m == 3:
                            wrap(2)
                            table_3(2)
                        if m == 4:
                            index(2)
                            points_sum(2)
                        if m == 5:
                            high_digit(2)
                            points_inv(2)
                        if m == 6:
                            both_digits(2)
                            points_out(2)
                        if m == 7:
                            table_out(2)
                    if b + 1 < B:
                        if m == (2 if b == 0 else 1):
                            attend(b + 1)
                        if m == (3 if b == 0 else 2):
                            add_attention(b + 1)
                        if m == 3:
                            stats2(b + 1)
                        if m == 5:
                            norm2(b + 1)
                        if m == 6:
                            x_lo(b + 1)
                        if m == 7:
                            best(b + 1)
                            chosen(b + 1)
                        if m == 8:
                            gates(b + 1)
                    if m == 4 and b >= 1:
                        emit(b - 1)
                    if b + 2 < B:
                        if m == 9:
                            hi_onehot(b + 2)
                        if m == 10:
                            lo_onehot(b + 2)
            gated(B * M - 1)
            emit(B - 1)

        @block.tensor
        def _(pe):
            def mm(o, l, r, start=True, stop=True):
                return nc.tensor.matmul(o, l, r, start=start, stop=stop)

            def channels(b):
                if b >= 2:
                    pe.wait_ge(xnT_ok, b - 1)
                for t in range(T):
                    pe.wait_ge(xn_ok, b * T + t + 1)
                    last = nc.tensor.transpose(ps_g[b % 2][:, t * P:(t + 1) * P], xn[:, b % 2 * T + t, :], ident[:, :])
                last.then_inc(xnp_ok, 1)

            def project(b):
                pe.wait_ge(xnT_ok, b + 1)
                u, o = PR_AT[b]
                if b == 2:
                    pe.wait_ge(cw_ok, 1)
                for t in range(T):
                    last = mm(u[:, o + t * 2 * HP:o + (t + 1) * 2 * HP], xnT[:, b, t * P:(t + 1) * P],
                              wcat[:, :])
                last.then_inc(prp_ok, 1)

            def table(i):
                b0, b1 = TURNS[i]
                pe.wait_ge(tv_ok, i + 1)
                if i >= 1:
                    pe.wait_ge(tr_ok, i)
                mm(ps_w[:, b0 * HI:b1 * HI], sel_lo[:, :],
                   tv[:, b0:b1, :].rearrange("p b a -> p (b a)")).then_inc(tp_ok, 1)

            def turn_lo(b):
                pe.wait_ge(lo_ok, turn(b) + 1)
                if b == 1:
                    pe.wait_ge(pr_ok, 2)
                if b >= 2:
                    pe.wait_ge(sc_ok, b)
                for t in range(T):
                    last = nc.tensor.transpose(DIGITS_AT[b][1][0:HP, t * 64:(t + 1) * 64].bitcast(bf16),
                                               lo[:, b * T + t, :], identb[:, :])
                last.then_inc(lop_ok, 1)

            def replicate(b, q0, q1):
                for q in range(q0, q1):
                    if q == 0:
                        pe.wait_ge(loT_ok, b + 1)
                        if b >= 2:
                            pe.wait_ge(xlo_ok, b)
                    if q >= 2:
                        pe.wait_ge(rep_ok, b * QL + q - 1)
                    mm(DIGITS_AT[b][q % 2][:, :], seat[:, q * JL:(q + 1) * JL, :].rearrange("k c b -> k (c b)"), loT[:, :]
                       ).then_inc(repp_ok, 1)

            def look(b):
                pe.wait_ge(oh_ok, b + 1)
                pe.wait_ge(tbd_ok, turn(b) + 1)
                if b >= 1:
                    pe.wait_ge(gT_ok, b)
                w = HI * JL
                for t in range(T):
                    for q in range(QL):
                        at = (t % 2) * QL * w + q * w
                        for i in range(PIECES):
                            last = mm(ps_s[t // 2][:, at:at + w], oh[:, q, t * P:(t + 1) * P],
                                      tbd[:, b, i, :, :].rearrange("p a j -> p (a j)"),
                                      start=(i == 0), stop=(i == PIECES - 1))
                    if t % 2 == 1:
                        last.then_inc(look_ok, 1)

            def turn_x(b):
                if b == 0:
                    pe.wait_ge(ss_ok, 1)
                if b >= 2:
                    pe.wait_ge(out_ok, b - 1)
                for t in range(T):
                    pe.wait_ge(xn2_ok, b * T + t + 1)
                    last = nc.tensor.transpose(ps_s[0][:, t * P:(t + 1) * P], xn2[:, t, :], ident[:, :])
                last.then_inc(xn2p_ok, 1)

            def scores(b):
                pe.wait_ge(xhi_ok, b + 1)
                pe.wait_ge(xlo_ok, b + 1)
                w2 = wgt2[:, :, :].rearrange("p k e -> p (k e)")
                for t in range(T):
                    at = slice(t * 2 * NE, (t + 1) * 2 * NE)
                    mm(ps_s[1][:, at], xhi[:, b % 2, t * P:(t + 1) * P], w2, start=True, stop=False)
                    last = mm(ps_s[1][:, at], xlo[:, b % 2, t * P:(t + 1) * P], w2, start=False, stop=True)
                last.then_inc(scp_ok, 1)

            def turn_g(b):
                pe.wait_ge(g2_ok, b + 1)
                if 1 <= b < B - 1:
                    pe.wait_ge(rep_ok, (b + 2) * QL)
                for t in range(T):
                    last = nc.tensor.transpose(ps_s[1][0:GK, t * P:(t + 1) * P],
                                               g2[:, t, :, :].rearrange("p k e -> p (k e)").bitcast(fp32),
                                               ident[:, :])
                last.then_inc(gTp_ok, 1)

            def turn_y(b):
                pe.wait_ge(y_ok, b + 1)
                if b + 2 < B:
                    pe.wait_ge(ss_ok, b + 3)
                if b == B - 1:
                    pe.wait_ge(out_ok, b)
                for t in range(T):
                    last = nc.tensor.transpose(ps_s[0][:, t * P:(t + 1) * P], ys[:, t * P:(t + 1) * P], ident[:, :])
                last.then_inc(yp_ok, 1)

            pe.wait_ge(ident_ok, 1)
            channels(0)
            pe.wait_ge(wcat_ok, 2)
            project(0)
            pe.wait_ge(sel_ok, 1)
            table(0)
            channels(1)
            pe.wait_ge(pool_c, 5)
            pe.wait_ge(ld_wo, 16)
            mm(ps_y[:, 0:C], ones[:, :], wo[:, :]).then_inc(cwp_ok, 1)
            project(1)
            pe.wait_ge(identb_ok, 1)
            turn_lo(0)
            pe.wait_ge(seat_ok, 1)
            replicate(0, 0, QL)
            look(0)
            channels(2)
            turn_lo(1)
            table(1)
            project(2)
            replicate(1, 0, 2)
            channels(3)
            replicate(1, 2, QL)
            turn_x(0)
            project(3)
            table(2)
            pe.wait_ge(wgt_ok, 2)
            scores(0)

            def down(j):
                c = j % M
                pe.wait_ge(hhi_ok, j + 1)
                if c == 0 and j > 0:
                    pe.wait_ge(y_ok, j // M)
                wh, wl = (w[:, 2, c * P:(c + 1) * P] for w in (whi, wlo))
                mm(ps_y[:, :], wh, hhi[:, j % NS, :], start=(c == 0), stop=False)
                mm(ps_y[:, :], wl, hhi[:, j % NS, :], start=False, stop=False)
                pe.wait_ge(hlo_ok, j + 1)
                mm(ps_y[:, :], wh, hlo[:, j % NS, :], start=False, stop=(c == M - 1)).then_inc(dn_ok, 1)

            def gate(k):
                if k == 0:
                    pe.wait_ge(spread_ok, 1)
                    pe.wait_ge(tr_ok, len(TURNS))
                else:
                    pe.wait_ge(gw_ok, k)
                pe.wait_ge(gT_ok, k // M + 1)
                m = k % M
                mm(ps_w[:, :], spread[:, m * P:(m + 1) * P], gT[:, k // M % 2, :]).then_inc(pw_ok, 1)

            for b in range(B):
                for m in range(M):
                    k = b * M + m
                    xh, xl = xhi[:, b % 2, :], xlo[:, b % 2, :]
                    cols = slice(m * P, (m + 1) * P)
                    for i, (ps, ok, free) in enumerate([(ps_g, pg_ok, sg_ok), (ps_u, pu_ok, su_ok)]):
                        if k >= 2:
                            pe.wait_ge(free, k - 1)
                        elif k == 0:
                            pe.wait_ge(wlo_ok, i + 1)
                        if i == 1 and k < 2:
                            pe.wait_ge(rep_ok, 2 * QL)
                        mm(ps[k % 2][:, :], whi[:, i, cols], xh, start=True, stop=False)
                        mm(ps[k % 2][:, :], wlo[:, i, cols], xh, start=False, stop=False)
                        mm(ps[k % 2][:, :], whi[:, i, cols], xl, start=False, stop=True).then_inc(ok, 1)
                    if k == 1:
                        turn_g(0)
                    if k == 2:
                        gate(0)
                        gate(1)
                    if k >= 2:
                        gate(k)
                    if k == LAG:
                        pe.wait_ge(wlo_ok, 3)
                        pe.wait_ge(pr_ok, 3)
                    if k >= LAG:
                        down(k - LAG)
                    if m == 3 and b >= 1:
                        turn_y(b - 1)
                    if b + 1 < B:
                        if m == (2 if b == 0 else 1):
                            look(b + 1)
                        if m == 6:
                            turn_x(b + 1)
                        if m == 7:
                            scores(b + 1)
                        if m == 10:
                            turn_g(b + 1)
                    if b + 2 < B:
                        if m == 7:
                            turn_lo(b + 2)
                        if m == 8:
                            replicate(b + 2, 0, 2)
                        if m == 9:
                            replicate(b + 2, 2, 4)
            for j in range(B * M - LAG, B * M):
                down(j)
            turn_y(B - 1)


_INS = ['L0_attn_x', 'L0_attn_W_off', 'L0_attn_b_off', 'L0_attn_W_attn', 'L0_attn_b_attn', 'L0_attn_W_out',
        'L0_attn_b_out', 'L0_ffn_w_gate', 'L0_ffn_w_g', 'L0_ffn_w_u', 'L0_ffn_w_d']


def kernel(**inputs):
    import numpy as _np
    import concourse.bacc as _bacc
    from concourse import mybir as _mybir
    from concourse.bass_utils import run_bass_kernel_spmd as _run

    nc = _bacc.Bacc("TRN2", target_bir_lowering=False, num_devices=1)
    arrays, args = {}, []
    for name in _INS:
        a = _np.ascontiguousarray(inputs[name])
        arrays[f"in_{name}_dram"] = a
        args.append(nc.dram_tensor(f"in_{name}_dram", a.shape, _mybir.dt.from_np(a.dtype), kind="ExternalInput").ap())
    shape = arrays[f"in_{_INS[0]}_dram"].shape
    args.append(nc.dram_tensor("out_0_dram", shape, _mybir.dt.float32, kind="ExternalOutput").ap())
    deform_attn_then_moe(nc, *args)
    r = _run(nc, [arrays], core_ids=[0])
    return r.results[0]["out_0_dram"]
```

```python
import concourse.bass as bass
from concourse import mybir
from contextlib import ExitStack




def deform_attn_then_moe(nc, x, w_off, b_off, w_attn, b_attn, w_out, b_out, w_gate, w_g, w_u, w_d, out):
    fp32, fp32r, bf16, i32 = (mybir.dt.float32, mybir.dt.float32r, mybir.dt.bfloat16, mybir.dt.int32)
    ALU = mybir.AluOpType
    ACT = mybir.ActivationFunctionType
    AX = mybir.AxisListType

    B, N, C = x.shape
    P = 128
    T = N // P
    NE, _, FM = w_g.shape
    HALL = NE * FM
    M = HALL // P
    HP = w_attn.shape[1]
    NP = 4
    NHD = HP // NP
    LO, HI = 16, C // 16
    JL = P // LO
    QL = HP // JL
    PIECES = 3
    GK = 2 * NE
    EPS = 1e-5
    LAG = 4
    NH = 3
    NS = 4

    w_g_v = w_g.rearrange("e d m -> d e m")
    w_u_v = w_u.rearrange("e d m -> d e m")
    w_d_v = w_d.rearrange("e m d -> (e m) d").rearrange("(c p) d -> p c d", p=P)

    ctx = ExitStack()
    with ctx:
        def sb(name, shape, dt=fp32):
            return ctx.enter_context(nc.sbuf_tensor(name, shape, dt))

        def sem(name):
            return ctx.enter_context(nc.semaphore(name))

        xs = sb("xs", [P, B * T, C])
        xb = sb("xb", [P, B * T, C])
        x2 = sb("x2", [P, B * T, C])
        wp = sb("wp", [P, 3 * HP])
        bp = sb("bp", [P, 3 * HP])
        wcat = sb("wcat", [P, 2 * HP])
        bcat = sb("bcat", [P, 2 * HP])
        wo = sb("wo", [P, C])
        bo = sb("bo", [P, C])
        cw = sb("cw", [P, C])
        wgt = sb("wgt", [P, NE])
        wgt2 = sb("wgt2", [P, 2, NE], fp32r)
        raw = sb("raw", [P, 3, HALL])
        whi = sb("whi", [P, 3, HALL], fp32r)
        wlo = sb("wlo", [P, 3, HALL], fp32r)
        ones = sb("ones", [P, P])
        ident = sb("ident", [P, P])
        identb = sb("identb", [P, P], bf16)
        part = sb("part", [P, 1], i32)
        bits = sb("bits", [P, 4], i32)
        col = sb("col", [P, 4])
        row_n = sb("row_n", [P, HP], i32)
        seat = sb("seat", [HP, QL * JL, LO], bf16)
        row_hi_i = sb("row_hi_i", [P, HI, JL], i32)
        row_hi = sb("row_hi", [P, HI, JL], bf16)
        rank_i = sb("rank_i", [P, NE], i32)
        rank = sb("rank", [P, NE])
        sel_lo = sb("sel_lo", [P, P])
        own = sb("own", [P, HI])
        spread = sb("spread", [GK, HALL], fp32r)
        minus_half = sb("minus_half", [P, B * T])
        st6 = sb("st6", [P, B * T, 6])
        mv = sb("mv", [P, B * T, 2])
        ve = sb("ve", [P, B * T])
        rs = sb("rs", [P, B * T])
        nb = sb("nb", [P, B * T])
        warm = sb("warm", [P, 1])
        xn = sb("xn", [P, 2 * T, C])
        xnT = sb("xnT", [P, B, N])
        pr = sb("pr", [P, B * T, 2 * HP])
        mx = sb("mx", [P, B * T, NHD])
        ex = sb("ex", [P, B * T, NHD, NP])
        sm = sb("sm", [P, B * T, NHD])
        wt = sb("wt", [P, B * T, HP])
        ia = sb("ia", [P, 2 * T, HP])
        ii = sb("ii", [P, 2 * T, HP], i32)
        ig = sb("ig", [P, 2 * T, HP])
        fl = sb("fl", [P, 2 * T, HP])
        ng = sb("ng", [P, 2 * T, HP])
        cc = sb("cc", [P, 2 * T, HP])
        ix = sb("ix", [P, 2 * T, HP], i32)
        ih = sb("ih", [P, 2 * T, HP], i32)
        lo = sb("lo", [P, B * T, HP], bf16)
        hi = sb("hi", [P, B * T, HP], bf16)
        tv = sb("tv", [P, B, HI])
        t3 = sb("t3", [P, B, PIECES, HI], bf16)
        tr = sb("tr", [P, B, 2, HI])
        tbd = sb("tbd", [P, B, PIECES, HI, JL], bf16)
        loT = sb("loT", [HP, N], bf16)
        rep = sb("rep", [P, QL, N], bf16)
        oh = sb("oh", [P, QL, N], bf16)
        eqh = sb("eqh", [P, T * QL, HI, JL], bf16)
        aw = sb("aw", [P, T * QL, HI, JL])
        junk = sb("junk", [P, T, QL * HI * JL])
        ss = sb("ss", [P, B * T])
        st6b = sb("st6b", [P, B * T, 6])
        mvb = sb("mvb", [P, B * T, 2])
        veb = sb("veb", [P, B * T])
        rsb = sb("rsb", [P, B * T])
        nbb = sb("nbb", [P, B * T])
        xn2 = sb("xn2", [P, T, C])
        xhi = sb("xhi", [P, 2, N], fp32r)
        xlo = sb("xlo", [P, 2, N], fp32r)
        sc = sb("sc", [P, T, NE])
        top = sb("top", [P, T, 8])
        tkey = sb("tkey", [P, T, 8])
        kgt = sb("kgt", [P, T, NE])
        keq = sb("keq", [P, T, NE])
        key = sb("key", [P, T, NE])
        one1 = sb("one1", [P, T, NE])
        both = sb("both", [P, T, NE])
        sign = sb("sign", [P, T, NE])
        gap = sb("gap", [P, T])
        th = sb("th", [P, T])
        gs = sb("gs", [P, T, NE])
        g2 = sb("g2", [P, T, 2, NE], fp32r)
        gT = sb("gT", [GK, 2, N], fp32r)
        sg = sb("sg", [P, 2, N])
        su = sb("su", [P, NH, N])
        hh = sb("hh", [P, NH, N])
        hhi = sb("hhi", [P, NS, N], fp32r)
        hlo = sb("hlo", [P, NS, N], fp32r)
        gw = sb("gw", [P, 2, N])
        ys = sb("ys", [P, N])

        def bank(name):
            return ctx.enter_context(nc.psum_tensor(name, [P, 512], fp32))

        ps_g = [bank("ps_g0"), bank("ps_g1")]
        ps_u = [bank("ps_u0"), bank("ps_u1")]
        ps_w, ps_y = bank("ps_w"), bank("ps_y")
        ps_s = [bank("ps_s0"), bank("ps_s1")]

        ld_x = [sem(f"ld_x{b}") for b in range(B)]
        ld_p, ld_wo, ld_bo, ld_wgt = map(sem, ["ld_p", "ld_wo", "ld_bo", "ld_wgt"])
        ld_w = [sem(f"ld_w{i}") for i in range(3)]
        st_out, hlo_last = sem("st_out"), sem("hlo_last")
        pool_c, ident_ok, identb_ok, sel_ok, seat_ok, spread_ok, wcat_ok, whi_ok, wlo_ok, cwp_ok, cw_ok, wgt_ok = map(
            sem, ["pool_c", "ident_ok", "identb_ok", "sel_ok", "seat_ok", "spread_ok", "wcat_ok", "whi_ok", "wlo_ok",
                  "cwp_ok", "cw_ok", "wgt_ok"])
        dve, pool = sem("dve"), sem("pool")
        (var_ok, rs_ok, nb_ok, pr_ok, sub_ok, exp_ok, tv_ok, tp_ok, tr_ok, tbd_ok, lo_ok, wt_ok) = map(sem, [
            "var_ok", "rs_ok", "nb_ok", "pr_ok", "sub_ok", "exp_ok", "tv_ok", "tp_ok", "tr_ok", "tbd_ok", "lo_ok", "wt_ok"])
        (hi_ok, xn_ok, xnp_ok, xnT_ok, prp_ok, xb_ok, eqh_ok, aw_ok, oh_ok, look_ok, ss_ok) = map(sem, [
            "hi_ok", "xn_ok", "xnp_ok", "xnT_ok", "prp_ok", "xb_ok", "eqh_ok", "aw_ok", "oh_ok", "look_ok", "ss_ok"])
        lop_ok, loT_ok = sem("lop_ok"), sem("loT_ok")
        repp_ok, rep_ok = sem("repp_ok"), sem("rep_ok")
        (varb_ok, rsb_ok, nbb_ok, xn2_ok, xn2p_ok, xhi_ok, xlo_ok, scp_ok, sc_ok, gap_ok, th_ok, g2_ok, gTp_ok,
         gT_ok, y_ok, yp_ok, out_ok) = map(sem, [
             "varb_ok", "rsb_ok", "nbb_ok", "xn2_ok", "xn2p_ok", "xhi_ok", "xlo_ok", "scp_ok", "sc_ok", "gap_ok",
             "th_ok", "g2_ok", "gTp_ok", "gT_ok", "y_ok", "yp_ok", "out_ok"])
        (pg_ok, pu_ok, pw_ok, gw_ok, sg_ok, su_ok, hh_ok, hhi_ok, hlo_ok, dn_ok) = map(sem, [
            "pg_ok", "pu_ok", "pw_ok", "gw_ok", "sg_ok", "su_ok", "hh_ok", "hhi_ok", "hlo_ok", "dn_ok"])

        TURNS = [(0, 1), (1, 2), (2, B)]
        PR_AT = {0: (ps_u[0], 0), 1: (ps_u[1], 0), 2: (ps_y, 0), 3: (ps_y, 256)}

        DIGITS_AT = {b: ps_s for b in range(B)}
        DIGITS_AT[1] = [ps_s[0], ps_s[0]]

        TURN_AT = {b: ps_s[1] for b in range(B)}
        TURN_AT[1] = ps_u[1]

        END = B * M - 1
        HALVES = [slice(h * N // 2, (h + 1) * N // 2) for h in range(2)]

        def bank_y(h):
            return ps_s[h or 0]

        def turn(b):
            return next(i for i, (b0, b1) in enumerate(TURNS) if b < b1)

        def tiles(b0, b1):
            return slice(b0 * T, b1 * T)

        block = ctx.enter_context(nc.Block())

        @block.sync
        def _(sp):
            xv = x.rearrange("b (t p) c -> b p t c", p=P)
            sp.dma_start(xs[:, 0:T, :], xv[0]).then_inc(ld_x[0], 16)
            sp.dma_start(wp[:, 0:2 * HP], w_off).then_inc(ld_p, 16)
            sp.dma_start(wp[:, 2 * HP:3 * HP], w_attn).then_inc(ld_p, 16)
            for b in range(1, B):
                sp.dma_start(xs[:, b * T:(b + 1) * T, :], xv[b]).then_inc(ld_x[b], 16)
            sp.dma_start(raw[:, 0, :].rearrange("p (e m) -> p e m", e=NE), w_g_v).then_inc(ld_w[0], 16)
            sp.dma_start(raw[:, 1, :].rearrange("p (e m) -> p e m", e=NE), w_u_v).then_inc(ld_w[1], 16)
            sp.dma_start(raw[:, 2, :].rearrange("p (c d) -> p c d", c=M), w_d_v).then_inc(ld_w[2], 16)
            ov = out.rearrange("b (t p) c -> b p t c", p=P)
            for b in range(B - 1):
                sp.wait_ge(out_ok, b + 1)
                sp.dma_start(ov[b], x2[:, b * T:(b + 1) * T, :]).then_inc(st_out, 16)
            for h in range(2):
                t = slice(h * T // 2, (h + 1) * T // 2)
                sp.wait_ge(out_ok, B + h)
                sp.dma_start(ov[B - 1][:, t, :], x2[:, (B - 1) * T + t.start:(B - 1) * T + t.stop, :]
                             ).then_inc(st_out, 16)
            sp.wait_ge(st_out, 16 * (B + 1))

        @block.gpsimd
        def _(eng):
            n = [0]

            def link(ins):
                n[0] += 1
                ins.then_inc(pool, 1)
                eng.wait_ge(pool, n[0])

            link(eng.memset(ident[:, :], 0.0))
            eng.affine_select(out=ident[:, :], in_=ident[:, :], compare_op=ALU.not_equal, fill=1.0, base=0,
                              pattern=[[-1, P]], channel_multiplier=1).then_inc(ident_ok, 1)
            eng.iota(part[:, :], pattern=[[0, 1]], base=0, channel_multiplier=1).then_inc(pool_c, 1)
            eng.iota(row_n[:, :], pattern=[[1, HP]], base=0, channel_multiplier=0).then_inc(pool_c, 1)
            eng.iota(row_hi_i[:, :, :], pattern=[[1, HI], [0, JL]], base=0, channel_multiplier=0).then_inc(pool_c, 1)
            eng.iota(rank_i[:, :], pattern=[[-1, NE]], base=NE, channel_multiplier=0).then_inc(pool_c, 1)
            eng.memset(ones[:, :], 1.0).then_inc(pool_c, 1)
            link(eng.memset(minus_half[:, :], -0.5))

            def rstd(v, m, r, t, ready, count, done):
                eng.wait_ge(ready, count)
                link(eng.tensor_scalar(v[:, t], m[:, t, 1], EPS, None, ALU.add))
                eng.tensor_tensor(r[:, t], v[:, t], minus_half[:, t], ALU.pow).then_inc(done, 1)

            def residual(b):
                t = tiles(b, b + 1)
                if b == 0:
                    eng.wait_ge(ld_bo, 16)
                eng.wait_ge(ld_x[b], 16)
                eng.tensor_tensor(xb[:, t, :], xs[:, t, :], bo[:, :].unsqueeze(1).to_broadcast([P, T, C]),
                                  ALU.add).then_inc(xb_ok, 1)

            def weights_lo(i):
                eng.wait_ge(whi_ok, i + 1)
                eng.tensor_tensor(wlo[:, i, :], raw[:, i, :], whi[:, i, :].bitcast(fp32), ALU.subtract
                                  ).then_inc(wlo_ok, 1)

            def weigh_hi(b):
                eng.wait_ge(eqh_ok, b + 1)
                eng.wait_ge(wt_ok, turn(b) + 1)
                if b >= 1:
                    eng.wait_ge(ss_ok, b)
                eng.tensor_tensor(aw[:, :, :, :], eqh[:, :, :, :],
                                  wt[:, tiles(b, b + 1), :].rearrange("p t (q j) -> p (t q) j", j=JL)
                                  .unsqueeze(2).to_broadcast([P, T * QL, HI, JL]), ALU.mult).then_inc(aw_ok, 1)

            rstd(ve, mv, rs, tiles(0, 1), var_ok, 1, rs_ok)
            residual(0)
            rstd(ve, mv, rs, tiles(1, 2), var_ok, 2, rs_ok)
            weights_lo(0)
            weigh_hi(0)
            rstd(ve, mv, rs, tiles(2, B), var_ok, 3, rs_ok)
            weights_lo(1)
            residual(1)
            rstd(veb, mvb, rsb, tiles(0, 1), varb_ok, 1, rsb_ok)
            weigh_hi(1)
            weights_lo(2)
            for b in range(B):
                for m in range(M):
                    k = b * M + m
                    if k == END:
                        break
                    eng.wait_ge(hhi_ok, k + 1)
                    if k >= NS:
                        eng.wait_ge(dn_ok, k - NS + 1)
                    at = HALVES[0] if k == END - 1 else slice(0, N)
                    eng.tensor_tensor(hlo[:, k % NS, at], hh[:, k % NH, at], hhi[:, k % NS, at].bitcast(fp32),
                                      ALU.subtract).then_inc(hlo_ok, 1)
                    if b + 1 < B:
                        if m == 2:
                            rstd(veb, mvb, rsb, tiles(b + 1, b + 2), varb_ok, b + 2, rsb_ok)
                    if b + 2 < B:
                        if m == 5:
                            residual(b + 2)
                        if m == 10:
                            weigh_hi(b + 2)

        @block.scalar
        def _(act):
            act.dma_start(bp[:, 0:2 * HP], b_off.partition_broadcast(P)).then_inc(ld_p, 16)
            act.dma_start(bp[:, 2 * HP:3 * HP], b_attn.partition_broadcast(P)).then_inc(ld_p, 16)
            act.dma_start(bo[:, :], b_out.partition_broadcast(P)).then_inc(ld_bo, 16)
            act.dma_start(wgt[:, :], w_gate).then_inc(ld_wgt, 16)
            act.dma_start(wo[:, :], w_out).then_inc(ld_wo, 16)
            A = nc.scalar.activation

            def channels(b):
                act.wait_ge(xnp_ok, b + 1)
                A(xnT[:, b, :], ps_g[b % 2][:, :], ACT.Copy).then_inc(xnT_ok, 1)

            def norm1(b):
                act.wait_ge(nb_ok, 1)
                act.wait_ge(xnp_ok, b - 1)
                for t in range(b * T, (b + 1) * T):
                    A(xn[:, t % (2 * T), :], xs[:, t, :], ACT.Identity, bias=nb[:, t:t + 1], scale=rs[:, t:t + 1]
                      ).then_inc(xn_ok, 1)

            def exps(i):
                t = tiles(*TURNS[i])
                act.wait_ge(sub_ok, i + 1)
                A(ex[:, t, :, :], ex[:, t, :, :], ACT.Exp).then_inc(exp_ok, 1)

            def weights_hi(i):
                act.wait_ge(ld_w[i], 16)
                A(whi[:, i, :], raw[:, i, :], ACT.Copy).then_inc(whi_ok, 1)

            def low_T(b):
                act.wait_ge(lop_ok, b + 1)
                if b >= 1:
                    act.wait_ge(repp_ok, QL * b)
                A(loT[:, :], TURN_AT[b][0:HP, 0:256].bitcast(bf16), ACT.Copy).then_inc(loT_ok, 1)

            def digits(b, q0, q1):
                for q in range(q0, q1):
                    act.wait_ge(repp_ok, b * QL + q + 1)
                    if b >= 1 and q == 0:
                        act.wait_ge(oh_ok, b)
                    A(rep[:, q, :], DIGITS_AT[b][q % 2][:, :], ACT.Copy).then_inc(rep_ok, 1)

            def norm2(b, h):
                act.wait_ge(nbb_ok, b)
                act.wait_ge(xn2p_ok, b)
                for t in range(b * T + h * T // 2, b * T + (h + 1) * T // 2):
                    A(xn2[:, t % T, :], x2[:, t, :], ACT.Identity, bias=nbb[:, t:t + 1], scale=rsb[:, t:t + 1]
                      ).then_inc(xn2_ok, 1)

            def x_hi(b):
                act.wait_ge(xn2p_ok, b + 1)
                if b >= 2:
                    act.wait_ge(pu_ok, M * (b - 1))
                A(xhi[:, b % 2, :], ps_s[0][:, :], ACT.Copy).then_inc(xhi_ok, 1)

            def split(b):
                act.wait_ge(gap_ok, b + 1)
                A(th[:, :], gap[:, :], ACT.Tanh, scale=0.5).then_inc(th_ok, 1)

            def gates_T(b):
                act.wait_ge(gTp_ok, b + 1)
                if b >= 2:
                    act.wait_ge(pw_ok, M * (b - 1))
                A(gT[:, b % 2, :], ps_s[1][0:GK, :], ACT.Copy).then_inc(gT_ok, 1)

            channels(0)
            weights_hi(0)
            channels(1)
            exps(0)
            low_T(0)
            digits(0, 0, QL)
            weights_hi(1)
            norm1(2)
            norm1(3)
            channels(2)
            channels(3)
            exps(1)
            weights_hi(2)
            x_hi(0)
            low_T(1)
            exps(2)
            act.wait_ge(ident_ok, 1)
            A(warm[:, :], ident[:, 0:1], ACT.Silu)
            digits(1, 0, 1)
            split(0)

            def high(j):
                act.wait_ge(hh_ok, j + 1)
                if j >= NS:
                    act.wait_ge(dn_ok, j - NS + 1)
                A(hhi[:, j % NS, :], hh[:, j % NH, :], ACT.Copy).then_inc(hhi_ok, 1)

            def y_out(b, halves=1):
                if b >= 1:
                    act.wait_ge(yp_ok, b)
                act.wait_ge(dn_ok, M * (b + 1))
                for h in range(halves):
                    c = slice(h * N // halves, (h + 1) * N // halves)
                    A(ys[:, c], ps_y[:, c], ACT.Copy).then_inc(y_ok, 1)

            def gate(j):
                act.wait_ge(pw_ok, j + 1)
                if j >= 2:
                    act.wait_ge(hh_ok, j - 1)
                A(gw[:, j % 2, :], ps_w[:, :], ACT.Copy).then_inc(gw_ok, 1)

            for b in range(B):
                for m in range(M):
                    k = b * M + m
                    act.wait_ge(pg_ok, k + 1)
                    if k >= 2:
                        act.wait_ge(su_ok, k - 1)
                    A(sg[:, k % 2, :], ps_g[k % 2][:, :], ACT.Silu).then_inc(sg_ok, 1)
                    if k < 3:
                        digits(1, k + 1, k + 2)
                    if k == 1:
                        gates_T(0)
                    if k == 2:
                        gate(0)
                        gate(1)
                    if 2 <= k < END:
                        gate(k)
                    if 2 <= k < B * M - 1:
                        high(k - 2)
                    if k >= B * M - 2:
                        high(k - 1)
                    if m == LAG - 1 and b >= 1:
                        y_out(b - 1)
                    if b + 1 < B:
                        if m == 0 and b >= 1:
                            digits(b + 1, 2, 4)
                        if m in (5, 6):
                            norm2(b + 1, m - 5)
                        if m == 7:
                            x_hi(b + 1)
                        if m == 9:
                            split(b + 1)
                        if m == 10:
                            gates_T(b + 1)
                    if b + 2 < B:
                        if m == 7:
                            low_T(b + 2)
                        if m == 9:
                            digits(b + 2, 0, 2)
            for h, at in enumerate(HALVES):
                act.wait_ge(hh_ok, END + 1 + h)
                act.wait_ge(dn_ok, END - NS + 1)
                A(hhi[:, END % NS, at], hh[:, END % NH, at], ACT.Copy).then_inc(hhi_ok, 1)
            y_out(B - 1, 2)

        @block.vector
        def _(eng):
            n = [0]
            V = nc.vector

            def did(ins):
                n[0] += 1
                ins.then_inc(dve, 1)
                return n[0]

            def after(step):
                eng.wait_ge(dve, step)

            def link(ins):
                after(did(ins))

            def stats(src, s6, m2, t0, t1):
                for t in range(t0, t1):
                    last = did(V.bn_stats(s6[:, t, :], src[:, t, :]))
                    if t > t0:
                        after(last - 2 if t > t0 + 1 else last - 1)
                        did(V.bn_aggr(m2[:, t - 1, :], s6[:, t - 1, :]))
                after(n[0] - 1)
                return V.bn_aggr(m2[:, t1 - 1, :], s6[:, t1 - 1, :])

            def normalise(dst, src, m2, r, b, done):
                for t in range(b * T, (b + 1) * T):
                    ins = V.tensor_scalar(dst[:, t % dst.shape[1], :], src[:, t, :], m2[:, t, 0:1], r[:, t:t + 1],
                                          ALU.subtract, ALU.mult)
                    ins.then_inc(done, 1)

            def neg_bias(nbias, m2, r, t, ready, count, done):
                eng.wait_ge(ready, count)
                V.scalar_tensor_tensor(out=nbias[:, t], in0=m2[:, t, 0], scalar=-1.0, in1=r[:, t],
                                       op0=ALU.mult, op1=ALU.mult).then_inc(done, 1)

            def norm1(b):
                eng.wait_ge(rs_ok, turn(b) + 1)
                normalise(xn, xs, mv, rs, b, xn_ok)

            def norm2(b):
                eng.wait_ge(rsb_ok, b + 1)
                normalise(xn2, x2, mvb, rsb, b, xn2_ok)

            def project(i):
                b0, b1 = TURNS[i]
                eng.wait_ge(prp_ok, b1)
                u, o = PR_AT[b0]
                nt = (b1 - b0) * T
                V.tensor_tensor(pr[:, tiles(b0, b1), :],
                                u[:, o:o + nt * 2 * HP].rearrange("p (t n) -> p t n", t=nt),
                                bcat[:, :].unsqueeze(1).to_broadcast([P, nt, 2 * HP]), ALU.add).then_inc(pr_ok, 1)
                eng.wait_ge(pr_ok, i + 1)

            step = {}

            def scratch(i):
                b0, b1 = TURNS[i]
                return slice(b0 % 2 * T, (b0 % 2 + b1 - b0) * T)

            def clamp(i):
                t, c = tiles(*TURNS[i]), scratch(i)
                step["cc"] = did(V.tensor_scalar(cc[:, c, :], pr[:, t, 0:HP], C - 1.0, -float(C), ALU.min, ALU.max))

            def magnitude(i):
                t, c = tiles(*TURNS[i]), scratch(i)
                after(step["cc"])
                step["ia"] = did(V.scalar_tensor_tensor(out=ia[:, c, :], in0=cc[:, c, :], scalar=-1.0,
                                                        in1=cc[:, c, :], op0=ALU.mult, op1=ALU.max))

            def to_int(i):
                t, c = tiles(*TURNS[i]), scratch(i)
                after(step["ia"])
                step["ii"] = did(V.tensor_copy(ii[:, c, :], ia[:, c, :]))
                step["ng"] = did(V.tensor_scalar(ng[:, c, :], cc[:, c, :], -1.0, -float(C), ALU.is_le, ALU.mult))

            def rounded_up(i):
                t, c = tiles(*TURNS[i]), scratch(i)
                after(step["ii"])
                step["ig"] = did(V.tensor_tensor(ig[:, c, :], ii[:, c, :], ia[:, c, :], ALU.is_gt))

            def wrap_by(i):
                t, c = tiles(*TURNS[i]), scratch(i)
                after(step["ng"])
                step["fl"] = did(V.tensor_tensor(fl[:, c, :], ii[:, c, :], ng[:, c, :], ALU.add))

            def wrap(i):
                t, c = tiles(*TURNS[i]), scratch(i)
                after(step["fl"])
                step["cc"] = did(V.tensor_tensor(cc[:, c, :], fl[:, c, :], ig[:, c, :], ALU.subtract))

            def index(i):
                t, c = tiles(*TURNS[i]), scratch(i)
                after(step["cc"])
                step["ix"] = did(V.scalar_tensor_tensor(out=ix[:, c, :], in0=cc[:, c, :], scalar=-1.0,
                                                        in1=cc[:, c, :], op0=ALU.mult, op1=ALU.max))

            def high_digit(i):
                t, c = tiles(*TURNS[i]), scratch(i)
                after(step["ix"])
                step["ih"] = did(V.tensor_scalar(ih[:, c, :], ix[:, c, :], 4, None, ALU.arith_shift_right))

            def both_digits(i):
                t, c = tiles(*TURNS[i]), scratch(i)
                after(step["ih"])
                V.scalar_tensor_tensor(out=lo[:, t, :], in0=ih[:, c, :], scalar=-float(LO), in1=ix[:, c, :],
                                       op0=ALU.mult, op1=ALU.add).then_inc(lo_ok, 1)
                V.tensor_copy(hi[:, t, :], ih[:, c, :]).then_inc(hi_ok, 1)

            def logits(t):
                return pr[:, t, HP:2 * HP].rearrange("p t (h q) -> p t h q", q=NP)

            def points_max(i):
                t = tiles(*TURNS[i])
                step["mx"] = did(V.tensor_reduce(mx[:, t, :], logits(t), AX.X, ALU.max))

            def points_sub(i):
                t = tiles(*TURNS[i])
                after(step["mx"])
                nt = t.stop - t.start
                V.tensor_tensor(ex[:, t, :, :], logits(t), mx[:, t, :].unsqueeze(3).to_broadcast([P, nt, NHD, NP]),
                                ALU.subtract).then_inc(sub_ok, 1)

            def points_sum(i):
                t = tiles(*TURNS[i])
                eng.wait_ge(exp_ok, i + 1)
                step["sm"] = did(V.tensor_reduce(sm[:, t, :], ex[:, t, :, :], AX.X, ALU.add))

            def points_inv(i):
                t = tiles(*TURNS[i])
                after(step["sm"])
                step["sm"] = did(V.reciprocal(sm[:, t, :], sm[:, t, :]))

            def points_out(i):
                t = tiles(*TURNS[i])
                after(step["sm"])
                nt = t.stop - t.start
                V.tensor_tensor(wt[:, t, :].rearrange("p t (h q) -> p t h q", q=NP), ex[:, t, :, :],
                                sm[:, t, :].unsqueeze(3).to_broadcast([P, nt, NHD, NP]), ALU.mult
                                ).then_inc(wt_ok, 1)

            def table_in(i):
                b0, b1 = TURNS[i]
                eng.wait_ge(xnT_ok, b1)
                V.tensor_tensor(tv[:, b0:b1, :], own[:, :].unsqueeze(1).to_broadcast([P, b1 - b0, HI]),
                                xnT[:, b0:b1, 0:1].to_broadcast([P, b1 - b0, HI]), ALU.mult).then_inc(tv_ok, 1)

            def table_got(i):
                b0, b1 = TURNS[i]
                eng.wait_ge(tp_ok, i + 1)
                V.tensor_copy(tr[:, b0:b1, 0, :], ps_w[:, b0 * HI:b1 * HI].rearrange("p (b a) -> p b a", a=HI)
                              ).then_inc(tr_ok, 1)

            def table_1(i):
                b0, b1 = TURNS[i]
                eng.wait_ge(tr_ok, i + 1)
                step["t1"] = did(V.tensor_copy(t3[:, b0:b1, 0, :], tr[:, b0:b1, 0, :]))

            def table_rest(i):
                b0, b1 = TURNS[i]
                after(step["t1"])
                step["tr1"] = did(V.tensor_tensor(tr[:, b0:b1, 1, :], tr[:, b0:b1, 0, :], t3[:, b0:b1, 0, :],
                                                  ALU.subtract))

            def table_2(i):
                b0, b1 = TURNS[i]
                after(step["tr1"])
                step["t2"] = did(V.tensor_copy(t3[:, b0:b1, 1, :], tr[:, b0:b1, 1, :]))

            def table_3(i):
                b0, b1 = TURNS[i]
                after(step["t2"])
                step["t3"] = did(V.tensor_tensor(t3[:, b0:b1, 2, :], tr[:, b0:b1, 1, :], t3[:, b0:b1, 1, :],
                                                 ALU.subtract))

            def table_out(i):
                b0, b1 = TURNS[i]
                after(step["t3"])
                k = (b1 - b0) * PIECES
                V.tensor_tensor(tbd[:, b0:b1, :, :, :].rearrange("p b k a j -> p (b k) a j"),
                                own[:, :].unsqueeze(1).unsqueeze(1).to_broadcast([P, k, HI, JL]),
                                t3[:, b0:b1, :, :].rearrange("p b k a -> p (b k) a").unsqueeze(3)
                                .to_broadcast([P, k, HI, JL]), ALU.mult).then_inc(tbd_ok, 1)

            def hi_onehot(b):
                eng.wait_ge(hi_ok, turn(b) + 1)
                if b >= 1:
                    eng.wait_ge(aw_ok, b)
                V.tensor_tensor(eqh[:, :, :, :], row_hi[:, :, :].unsqueeze(1).to_broadcast([P, T * QL, HI, JL]),
                                hi[:, tiles(b, b + 1), :].rearrange("p t (q j) -> p (t q) j", j=JL)
                                .unsqueeze(2).to_broadcast([P, T * QL, HI, JL]), ALU.is_equal).then_inc(eqh_ok, 1)

            def lo_onehot(b):
                eng.wait_ge(rep_ok, QL * (b + 1))
                if b >= 1:
                    eng.wait_ge(look_ok, b * T // 2)
                V.tensor_scalar(oh[:, :, :], rep[:, :, :], col[:, 0:1], None, ALU.is_equal).then_inc(oh_ok, 1)

            def attend(b):
                eng.wait_ge(aw_ok, b + 1)
                w = QL * HI * JL
                for t in range(T):
                    if t % 2 == 0:
                        eng.wait_ge(look_ok, b * T // 2 + t // 2 + 1)
                    ins = V.tensor_tensor_reduce(junk[:, t, :], aw[:, t * QL:(t + 1) * QL, :, :]
                                                 .rearrange("p q a j -> p (q a j)"),
                                                 ps_s[t // 2][:, t % 2 * w:(t % 2 + 1) * w], 1.0, 0.0,
                                                 ALU.mult, ALU.add, ss[:, b * T + t:b * T + t + 1])
                ins.then_inc(ss_ok, 1)

            def add_attention(b):
                eng.wait_ge(ss_ok, b + 1)
                eng.wait_ge(xb_ok, b + 1)
                for u in range(b * T, (b + 1) * T):
                    ins = did(V.scalar_tensor_tensor(out=x2[:, u, :], in0=cw[:, :], scalar=ss[:, u:u + 1],
                                                     in1=xb[:, u, :], op0=ALU.mult, op1=ALU.add))
                step["x2"] = ins

            def stats2(b):
                after(step["x2"])
                stats(x2, st6b, mvb, b * T, (b + 1) * T).then_inc(varb_ok, 1)

            def x_lo(b):
                eng.wait_ge(xhi_ok, b + 1)
                if b >= 2:
                    eng.wait_ge(pu_ok, M * (b - 1))
                V.tensor_tensor(xlo[:, b % 2, :], ps_s[0][:, :], xhi[:, b % 2, :].bitcast(fp32), ALU.subtract
                                ).then_inc(xlo_ok, 1)

            def wide(v):
                return v.unsqueeze(2).to_broadcast([P, T, NE])

            def best(b):
                eng.wait_ge(scp_ok, b + 1)
                V.tensor_reduce(sc[:, :, :], ps_s[1][:, 0:T * 2 * NE].rearrange("p (t k e) -> p t e k", t=T, k=2),
                                AX.X, ALU.add).then_inc(sc_ok, 1)
                eng.wait_ge(sc_ok, b + 1)
                for t in range(T):
                    ins = V.max(top[:, t, :], sc[:, t, :])
                link(ins)
                V.tensor_tensor(gap[:, :], top[:, :, 0], top[:, :, 1], ALU.subtract).then_inc(gap_ok, 1)
                s1 = did(V.tensor_tensor(keq[:, :, :], sc[:, :, :], wide(top[:, :, 1]), ALU.is_equal))
                did(V.tensor_tensor(kgt[:, :, :], sc[:, :, :], wide(top[:, :, 1]), ALU.is_gt))
                after(s1)
                link(V.tensor_tensor(keq[:, :, :], keq[:, :, :], rank[:, :].unsqueeze(1).to_broadcast([P, T, NE]),
                                     ALU.mult))
                link(V.scalar_tensor_tensor(out=key[:, :, :], in0=kgt[:, :, :], scalar=2.0 * NE, in1=keq[:, :, :],
                                            op0=ALU.mult, op1=ALU.add))
                for t in range(T):
                    ins = V.max(tkey[:, t, :], key[:, t, :])
                link(ins)

            def chosen(b):
                did(V.tensor_tensor(both[:, :, :], key[:, :, :], wide(tkey[:, :, 1]), ALU.is_ge))
                link(V.tensor_tensor(one1[:, :, :], key[:, :, :], wide(tkey[:, :, 0]), ALU.is_ge))
                step["sign"] = did(V.scalar_tensor_tensor(out=sign[:, :, :], in0=one1[:, :, :], scalar=2.0,
                                                          in1=both[:, :, :], op0=ALU.mult, op1=ALU.subtract))

            def gates(b):
                eng.wait_ge(th_ok, b + 1)
                after(step["sign"])
                link(V.tensor_tensor(gs[:, :, :], sign[:, :, :], wide(th[:, :]), ALU.mult))
                link(V.tensor_tensor(gs[:, :, :], gs[:, :, :], both[:, :, :], ALU.add))
                if b >= 1:
                    eng.wait_ge(gTp_ok, b)
                link(V.tensor_scalar(g2[:, :, 0, :], gs[:, :, :], 0.5, None, ALU.mult))
                V.scalar_tensor_tensor(out=g2[:, :, 1, :], in0=gs[:, :, :], scalar=0.5,
                                       in1=g2[:, :, 0, :].bitcast(fp32), op0=ALU.mult, op1=ALU.subtract
                                       ).then_inc(g2_ok, 1)

            def stats1(b):
                eng.wait_ge(ld_x[b], 16)
                return stats(xs, st6, mv, b * T, (b + 1) * T)

            stats1(0).then_inc(var_ok, 1)
            eng.wait_ge(pool_c, 4)
            eng.wait_ge(ident_ok, 1)
            for i, (op, v) in enumerate([(ALU.bitwise_and, LO - 1), (ALU.bitwise_and, NE - 1),
                                         (ALU.arith_shift_right, 4), (ALU.arith_shift_right, 0)]):
                ins = V.tensor_scalar(bits[:, i:i + 1], part[:, :], v, None, op)
            cast = did(ins)
            did(V.tensor_copy(rank[:, :], rank_i[:, :]))
            did(V.tensor_copy(row_hi[:, :, :], row_hi_i[:, :, :]))
            after(cast)
            link(V.tensor_copy(col[:, :], bits[:, :]))
            eng.wait_ge(ld_p, 64)
            V.tensor_copy(wcat[:, 0:HP], wp[:, 0:2 * HP:2]).then_inc(wcat_ok, 1)
            V.tensor_copy(wcat[:, HP:2 * HP], wp[:, 2 * HP:3 * HP]).then_inc(wcat_ok, 1)
            V.tensor_copy(identb[:, :], ident[:, :]).then_inc(identb_ok, 1)
            V.tensor_scalar(seat[:, :, :], row_n[0:HP, :].unsqueeze(2).to_broadcast([HP, QL * JL, LO]),
                            col[0:HP, 3:4], None, ALU.is_equal).then_inc(seat_ok, 1)
            norm1(0)
            stats1(1).then_inc(var_ok, 1)
            did(V.tensor_copy(bcat[:, 0:HP], bp[:, 0:2 * HP:2]))
            did(V.tensor_copy(bcat[:, HP:2 * HP], bp[:, 2 * HP:3 * HP]))
            link(V.tensor_scalar(own[:, :], row_hi_i[:, :, 0], col[:, 2:3], None, ALU.is_equal))
            V.tensor_scalar(sel_lo[:, :].rearrange("p (j b) -> p j b", b=LO),
                            row_n[:, 0:LO].unsqueeze(1).to_broadcast([P, JL, LO]), col[:, 0:1], None,
                            ALU.is_equal).then_inc(sel_ok, 1)
            table_in(0)
            norm1(1)
            project(0)
            clamp(0)
            points_max(0)
            magnitude(0)
            points_sub(0)
            to_int(0)
            table_got(0)
            rounded_up(0)
            table_1(0)
            wrap_by(0)
            wrap(0)
            table_rest(0)
            index(0)
            table_2(0)
            high_digit(0)
            table_3(0)
            both_digits(0)
            points_sum(0)
            hi_onehot(0)
            points_inv(0)
            table_out(0)
            points_out(0)
            did(stats1(2))
            stats1(3).then_inc(var_ok, 1)
            lo_onehot(0)
            project(1)
            clamp(1)
            points_max(1)
            magnitude(1)
            points_sub(1)
            to_int(1)
            neg_bias(nb, mv, rs, tiles(2, B), rs_ok, 3, nb_ok)
            table_in(1)
            V.tensor_copy(cw[:, :], ps_y[:, 0:C]).then_inc(cw_ok, 1)
            rounded_up(1)
            attend(0)
            eng.wait_ge(cw_ok, 1)
            add_attention(0)
            stats2(0)
            wrap_by(1)
            eng.wait_ge(ld_wgt, 16)
            V.tensor_copy(wgt2[:, 0, :], wgt[:, :]).then_inc(wgt_ok, 1)
            wrap(1)
            table_got(1)
            index(1)
            eng.wait_ge(wgt_ok, 1)
            V.tensor_tensor(wgt2[:, 1, :], wgt[:, :], wgt2[:, 0, :].bitcast(fp32), ALU.subtract).then_inc(wgt_ok, 1)
            table_in(2)
            high_digit(1)
            points_sum(1)
            norm2(0)
            both_digits(1)
            project(2)
            points_max(2)
            x_lo(0)
            points_sub(2)
            points_inv(1)
            table_1(1)
            table_rest(1)
            points_out(1)
            table_2(1)
            hi_onehot(1)
            table_3(1)
            table_out(1)
            best(0)
            chosen(0)
            table_got(2)

            def emit(b, h=None):
                t0, t1 = (0, T) if h is None else (h * T // 2, (h + 1) * T // 2)
                t = slice(b * T + t0, b * T + t1)
                eng.wait_ge(yp_ok, b + 1 + (h or 0))
                V.tensor_tensor(x2[:, t, :], bank_y(h)[:, t0 * C:t1 * C].rearrange("p (t c) -> p t c", c=C),
                                x2[:, t, :], ALU.add).then_inc(out_ok, 1)

            def up(k):
                eng.wait_ge(sg_ok, k + 1)
                eng.wait_ge(pu_ok, k + 1)
                V.tensor_tensor(su[:, k % NH, :], sg[:, k % 2, :], ps_u[k % 2][:, :], ALU.mult).then_inc(su_ok, 1)

            def gated(k):
                eng.wait_ge(su_ok, k + 1)
                eng.wait_ge(gw_ok, k + 1)
                if k >= NH:
                    eng.wait_ge(hlo_ok, k - NH + 1)
                V.tensor_tensor(hh[:, k % NH, :], su[:, k % NH, :], gw[:, k % 2, :], ALU.mult).then_inc(hh_ok, 1)

            for b in range(B):
                for m in range(M):
                    k = b * M + m
                    if k >= 3:
                        gated(k - 1)
                    up(k)
                    if k == 0:
                        gates(0)
                        V.tensor_scalar(spread[:, :].rearrange("k (e m) -> k e m", e=NE),
                                        row_n[0:GK, 0:NE].unsqueeze(2).to_broadcast([GK, NE, FM]), col[0:GK, 1:2], None,
                                        ALU.is_equal).then_inc(spread_ok, 1)
                    if k == 1:
                        lo_onehot(1)
                        clamp(2)
                    if k == 2:
                        gated(0)
                        gated(1)
                    if b == 0:
                        if m == 1:
                            magnitude(2)
                            to_int(2)
                        if m == 4:
                            rounded_up(2)
                            wrap_by(2)
                        if m == 5:
                            wrap(2)
                            index(2)
                        if m == 6:
                            high_digit(2)
                            both_digits(2)
                        if m == 8:
                            table_1(2)
                            points_sum(2)
                        if m == 9:
                            table_rest(2)
                            points_inv(2)
                            table_2(2)
                        if m == 10:
                            points_out(2)
                            table_3(2)
                            table_out(2)
                    if b + 1 < B:
                        if m == 2:
                            attend(b + 1)
                        if m == 3:
                            add_attention(b + 1)
                            stats2(b + 1)
                        if m == 4:
                            neg_bias(nbb, mvb, rsb, tiles(b + 1, b + 2), rsb_ok, b + 2, nbb_ok)
                        if m == 7:
                            x_lo(b + 1)
                        if m == 8:
                            best(b + 1)
                            chosen(b + 1)
                        if m == 9:
                            gates(b + 1)
                    if m == LAG + 1 and b >= 1:
                        emit(b - 1)
                    if 1 <= b < B - 1 and m == 1:
                        lo_onehot(b + 1)
                    if b + 2 < B:
                        if m == 9:
                            hi_onehot(b + 2)
            for h, at in enumerate(HALVES):
                eng.wait_ge(su_ok, END + 1)
                eng.wait_ge(pw_ok, END + 1)
                eng.wait_ge(hlo_ok, END - NH + 1)
                V.tensor_tensor(hh[:, END % NH, at], su[:, END % NH, at], ps_w[:, at], ALU.mult).then_inc(hh_ok, 1)
            k, at = END - 1, HALVES[1]
            eng.wait_ge(hhi_ok, k + 1)
            eng.wait_ge(dn_ok, k - NS + 1)
            V.tensor_tensor(hlo[:, k % NS, at], hh[:, k % NH, at], hhi[:, k % NS, at].bitcast(fp32), ALU.subtract
                            ).then_inc(hlo_last, 1)
            for h, at in enumerate(HALVES):
                eng.wait_ge(hhi_ok, END + 1 + h)
                eng.wait_ge(dn_ok, END - NS + 1)
                V.tensor_tensor(hlo[:, END % NS, at], hh[:, END % NH, at], hhi[:, END % NS, at].bitcast(fp32),
                                ALU.subtract).then_inc(hlo_last, 1)
            emit(B - 1, 0)
            emit(B - 1, 1)

        @block.tensor
        def _(pe):
            def mm(o, l, r, start=True, stop=True):
                return nc.tensor.matmul(o, l, r, start=start, stop=stop)

            def channels(b):
                if b >= 2:
                    pe.wait_ge(xnT_ok, b - 1)
                for t in range(T):
                    pe.wait_ge(xn_ok, b * T + t + 1)
                    last = nc.tensor.transpose(ps_g[b % 2][:, t * P:(t + 1) * P], xn[:, b % 2 * T + t, :], ident[:, :])
                last.then_inc(xnp_ok, 1)

            def project(b):
                pe.wait_ge(xnT_ok, b + 1)
                u, o = PR_AT[b]
                if b == 2:
                    pe.wait_ge(cw_ok, 1)
                for t in range(T):
                    last = mm(u[:, o + t * 2 * HP:o + (t + 1) * 2 * HP], xnT[:, b, t * P:(t + 1) * P],
                              wcat[:, :])
                last.then_inc(prp_ok, 1)

            def table(i):
                b0, b1 = TURNS[i]
                pe.wait_ge(tv_ok, i + 1)
                if i >= 1:
                    pe.wait_ge(tr_ok, i)
                mm(ps_w[:, b0 * HI:b1 * HI], sel_lo[:, :],
                   tv[:, b0:b1, :].rearrange("p b a -> p (b a)")).then_inc(tp_ok, 1)

            def turn_lo(b):
                pe.wait_ge(lo_ok, turn(b) + 1)
                if b == 1:
                    pe.wait_ge(pr_ok, 2)
                if b >= 2:
                    pe.wait_ge(ss_ok, b)
                for t in range(T):
                    last = nc.tensor.transpose(TURN_AT[b][0:HP, t * 64:(t + 1) * 64].bitcast(bf16),
                                               lo[:, b * T + t, :], identb[:, :])
                last.then_inc(lop_ok, 1)

            def replicate(b, q0, q1):
                for q in range(q0, q1):
                    if q == 0:
                        pe.wait_ge(loT_ok, b + 1)
                        if b >= 1:
                            pe.wait_ge(xlo_ok, b)
                    if b >= 2 and q == 1:
                        pe.wait_ge(sc_ok, b)
                    if b == 1 and q >= 1:
                        pe.wait_ge(rep_ok, QL + q)
                    elif b >= 2 and q == 3:
                        pe.wait_ge(gT_ok, b)
                    elif q >= 2:
                        pe.wait_ge(rep_ok, b * QL + q - 1)
                    mm(DIGITS_AT[b][q % 2][:, :], seat[:, q * JL:(q + 1) * JL, :].rearrange("k c b -> k (c b)"), loT[:, :]
                       ).then_inc(repp_ok, 1)

            def look(b):
                pe.wait_ge(oh_ok, b + 1)
                pe.wait_ge(tbd_ok, turn(b) + 1)
                if b == 1:
                    pe.wait_ge(gT_ok, 1)
                w = HI * JL
                for t in range(T):
                    for q in range(QL):
                        at = (t % 2) * QL * w + q * w
                        for i in range(PIECES):
                            last = mm(ps_s[t // 2][:, at:at + w], oh[:, q, t * P:(t + 1) * P],
                                      tbd[:, b, i, :, :].rearrange("p a j -> p (a j)"),
                                      start=(i == 0), stop=(i == PIECES - 1))
                    if t % 2 == 1:
                        last.then_inc(look_ok, 1)

            def turn_x(b):
                if b == 0:
                    pe.wait_ge(ss_ok, 1)
                if b >= 2:
                    pe.wait_ge(out_ok, b - 1)
                for t in range(T):
                    pe.wait_ge(xn2_ok, b * T + t + 1)
                    last = nc.tensor.transpose(ps_s[0][:, t * P:(t + 1) * P], xn2[:, t, :], ident[:, :])
                last.then_inc(xn2p_ok, 1)

            def scores(b):
                pe.wait_ge(xhi_ok, b + 1)
                pe.wait_ge(xlo_ok, b + 1)
                if 1 <= b < B - 1:
                    pe.wait_ge(loT_ok, b + 2)
                w2 = wgt2[:, :, :].rearrange("p k e -> p (k e)")
                for t in range(T):
                    at = slice(t * 2 * NE, (t + 1) * 2 * NE)
                    mm(ps_s[1][:, at], xhi[:, b % 2, t * P:(t + 1) * P], w2, start=True, stop=False)
                    last = mm(ps_s[1][:, at], xlo[:, b % 2, t * P:(t + 1) * P], w2, start=False, stop=True)
                last.then_inc(scp_ok, 1)

            def turn_g(b):
                pe.wait_ge(g2_ok, b + 1)
                if 1 <= b < B - 1:
                    pe.wait_ge(rep_ok, (b + 1) * QL + 2)
                for t in range(T):
                    last = nc.tensor.transpose(ps_s[1][0:GK, t * P:(t + 1) * P],
                                               g2[:, t, :, :].rearrange("p k e -> p (k e)").bitcast(fp32),
                                               ident[:, :])
                last.then_inc(gTp_ok, 1)

            def turn_y(b, h=None):
                pe.wait_ge(y_ok, b + 1 + (h or 0))
                if b + 2 < B:
                    pe.wait_ge(ss_ok, b + 3)
                if b == B - 1:
                    pe.wait_ge(out_ok, b)
                for t in range(T) if h is None else range(h * T // 2, (h + 1) * T // 2):
                    last = nc.tensor.transpose(bank_y(h)[:, t * P:(t + 1) * P], ys[:, t * P:(t + 1) * P], ident[:, :])
                last.then_inc(yp_ok, 1)

            pe.wait_ge(ident_ok, 1)
            channels(0)
            pe.wait_ge(wcat_ok, 2)
            project(0)
            pe.wait_ge(sel_ok, 1)
            table(0)
            channels(1)
            pe.wait_ge(pool_c, 5)
            pe.wait_ge(ld_wo, 16)
            mm(ps_y[:, 0:C], ones[:, :], wo[:, :]).then_inc(cwp_ok, 1)
            project(1)
            pe.wait_ge(identb_ok, 1)
            turn_lo(0)
            pe.wait_ge(seat_ok, 1)
            replicate(0, 0, QL)
            look(0)
            channels(2)
            table(1)
            channels(3)
            project(2)
            project(3)
            turn_x(0)
            table(2)
            turn_lo(1)

            def down(j):
                c = j % M
                pe.wait_ge(hhi_ok, j + 1)
                if c == 0 and j > 0:
                    pe.wait_ge(y_ok, j // M)
                wh, wl = (w[:, 2, c * P:(c + 1) * P] for w in (whi, wlo))
                mm(ps_y[:, :], wh, hhi[:, j % NS, :], start=(c == 0), stop=False)
                mm(ps_y[:, :], wl, hhi[:, j % NS, :], start=False, stop=False)
                pe.wait_ge(hlo_ok, j + 1)
                if j == END - 1:
                    pe.wait_ge(hlo_last, 1)
                mm(ps_y[:, :], wh, hlo[:, j % NS, :], start=False, stop=(c == M - 1)).then_inc(dn_ok, 1)

            def gate(k):
                if k == 0:
                    pe.wait_ge(spread_ok, 1)
                    pe.wait_ge(tr_ok, len(TURNS))
                else:
                    pe.wait_ge(gw_ok, k)
                pe.wait_ge(gT_ok, k // M + 1)
                m = k % M
                mm(ps_w[:, :], spread[:, m * P:(m + 1) * P], gT[:, k // M % 2, :]).then_inc(pw_ok, 1)

            for b in range(B):
                for m in range(M):
                    k = b * M + m
                    xh, xl = xhi[:, b % 2, :], xlo[:, b % 2, :]
                    cols = slice(m * P, (m + 1) * P)
                    for i, (ps, ok, free) in enumerate([(ps_g, pg_ok, sg_ok), (ps_u, pu_ok, su_ok)]):
                        if k >= 2:
                            pe.wait_ge(free, k - 1)
                        elif k == 0:
                            pe.wait_ge(wlo_ok, i + 1)
                        if i == 1 and k < 2:
                            pe.wait_ge(loT_ok, 2)
                        if k == 0 and i == 0:
                            pe.wait_ge(xhi_ok, 1)
                        mm(ps[k % 2][:, :], whi[:, i, cols], xh, start=True, stop=False)
                        mm(ps[k % 2][:, :], wlo[:, i, cols], xh, start=False, stop=False)
                        if k == 0 and i == 0:
                            pe.wait_ge(xlo_ok, 1)
                        mm(ps[k % 2][:, :], whi[:, i, cols], xl, start=False, stop=True).then_inc(ok, 1)
                        if k == 0 and i == 0:
                            pe.wait_ge(wgt_ok, 2)
                            scores(0)
                        if k < 2:
                            replicate(1, 2 * k + i, 2 * k + i + 1)
                        if k == 2 and i == 0:
                            gate(0)
                    if k == 1:
                        turn_g(0)
                    if k == 2:
                        gate(1)
                    if k >= 3:
                        gate(k)
                    if k == LAG:
                        pe.wait_ge(wlo_ok, 3)
                        pe.wait_ge(pr_ok, 3)
                    if k >= LAG:
                        down(k - LAG)
                    if m == LAG and b >= 1:
                        turn_y(b - 1)
                    if b + 1 < B:
                        if m == 0 and b >= 1:
                            replicate(b + 1, 2, 4)
                        if m == 2:
                            look(b + 1)
                            if k == 2:
                                gate(2)
                        if m == 7:
                            turn_x(b + 1)
                        if m == 8:
                            scores(b + 1)
                        if m == 10:
                            turn_g(b + 1)
                    if b + 2 < B:
                        if m == 7:
                            turn_lo(b + 2)
                        if m == 9:
                            replicate(b + 2, 0, 2)
            for j in range(B * M - LAG, END):
                down(j)
            wh, wl = (w[:, 2, (M - 1) * P:M * P] for w in (whi, wlo))
            for h, at in enumerate(HALVES):
                pe.wait_ge(hhi_ok, END + 1 + h)
                mm(ps_y[:, at], wh, hhi[:, END % NS, at], start=False, stop=False)
                mm(ps_y[:, at], wl, hhi[:, END % NS, at], start=False, stop=False)
            for h, at in enumerate(HALVES):
                pe.wait_ge(hlo_last, h + 2)
                last = mm(ps_y[:, at], wh, hlo[:, END % NS, at], start=False, stop=(h == 1))
            last.then_inc(dn_ok, 1)
            turn_y(B - 1, 0)
            turn_y(B - 1, 1)


_INS = ['L0_attn_x', 'L0_attn_W_off', 'L0_attn_b_off', 'L0_attn_W_attn', 'L0_attn_b_attn', 'L0_attn_W_out',
        'L0_attn_b_out', 'L0_ffn_w_gate', 'L0_ffn_w_g', 'L0_ffn_w_u', 'L0_ffn_w_d']


def kernel(**inputs):
    import numpy as _np
    import concourse.bacc as _bacc
    from concourse import mybir as _mybir
    from concourse.bass_utils import run_bass_kernel_spmd as _run

    nc = _bacc.Bacc("TRN2", target_bir_lowering=False, num_devices=1)
    arrays, args = {}, []
    for name in _INS:
        a = _np.ascontiguousarray(inputs[name])
        arrays[f"in_{name}_dram"] = a
        args.append(nc.dram_tensor(f"in_{name}_dram", a.shape, _mybir.dt.from_np(a.dtype), kind="ExternalInput").ap())
    shape = arrays[f"in_{_INS[0]}_dram"].shape
    args.append(nc.dram_tensor("out_0_dram", shape, _mybir.dt.float32, kind="ExternalOutput").ap())
    deform_attn_then_moe(nc, *args)
    r = _run(nc, [arrays], core_ids=[0])
    return r.results[0]["out_0_dram"]
```
